# Optimizing a Trainium2 kernel written in Bass

```python
import numpy as np
import jax
import jax.numpy as jnp

def _softmax(x, axis=-1):
    return jax.nn.softmax(x, axis=axis)

def _gelu(x):
    return jax.nn.gelu(x, approximate=True)

def _silu(x):
    return jax.nn.silu(x)

def _sigmoid(x):
    return jax.nn.sigmoid(x)

def _layernorm(x, axis=-1, eps=1e-05):
    m = jnp.mean(x, axis=axis, keepdims=True)
    v = jnp.var(x, axis=axis, keepdims=True)
    return (x - m) / jnp.sqrt(v + eps)

def _scatter_add(tgt, idx, src, axis=0):
    return tgt.at[idx].add(src)

def _segment_sum(src, seg, n):
    return jax.ops.segment_sum(src, seg, n)
kernel_name = 'mk_early_fusion_d2_tok_img768_r4_3fa488'

def setup_inputs(seed: int=0):
    np.random.seed(seed)
    _w = jnp.asarray

    def _rec_inputs():
        import jax
        import jax.numpy as jnp
        _rk = jax.random.key(seed)
        x = -0.000125008 + 0.999885 * jax.random.normal(jax.random.fold_in(_rk, 1), (16, 1, 224, 224), jnp.float32)
        txt = 3.85875e-05 + 0.319609 * jax.random.normal(jax.random.fold_in(_rk, 2), (16, 128, 192), jnp.float32)
        return (x, txt)
    x, txt = _rec_inputs()

    def _L0_tok_setup():
        import jax, jax.numpy as jnp
        import numpy as np
        PATCH = 16
        LATENT = 192

        def _extract_patches(x, p):
            B, C, H, W_ = x.shape
            nh, nw = (H // p, W_ // p)
            patches = x.reshape(B, C, nh, p, nw, p).transpose(0, 1, 2, 4, 3, 5)
            return patches.reshape(B, nh * nw, C * p * p)
        key = jax.random.key(seed)
        k1, k2 = jax.random.split(key)
        x = jax.random.normal(k1, (32, 1, 256, 256), dtype=jnp.float32)
        W = jax.random.normal(k2, (LATENT, PATCH * PATCH), dtype=jnp.float32) * 0.02
        return {'x': x, 'W': W}
    _L0_tok_all = _L0_tok_setup()
    _L0_tok_in = {k: v for k, v in _L0_tok_all.items() if k in ('W',)}
    del _L0_tok_all

    def _L0_attn_setup():
        import jax, jax.numpy as jnp
        import numpy as np
        DIM = 192
        NUM_HEADS = 12
        HEAD_DIM = DIM // NUM_HEADS
        key = jax.random.key(seed)
        k_x, k_a, k_v, k_p, k_b = jax.random.split(key, 5)
        B, N = (4, 512)
        s = 0.02
        return {'x': jax.random.normal(k_x, (B, N, DIM), dtype=jnp.float32), 'W_A': jax.random.normal(k_a, (DIM, NUM_HEADS), dtype=jnp.float32) * s, 'W_V': jax.random.normal(k_v, (DIM, DIM), dtype=jnp.float32) * s, 'W_proj': jax.random.normal(k_p, (DIM, DIM), dtype=jnp.float32) * s, 'b_proj': jax.random.normal(k_b, (DIM,), dtype=jnp.float32) * s}
    _L0_attn_all = _L0_attn_setup()
    _L0_attn_in = {k: v for k, v in _L0_attn_all.items() if k in ('W_A', 'W_V', 'W_proj', 'b_proj')}
    del _L0_attn_all

    def _L0_ffn_setup():
        import jax, jax.numpy as jnp
        import numpy as np
        B, S, D_IN, D_HID, D_OUT = (32, 128, 192, 768, 192)
        key = jax.random.key(seed)
        k1, k2, k3, k4 = jax.random.split(key, 4)
        init_k = float(np.sqrt(1.0 / D_IN))
        init_k2 = float(np.sqrt(1.0 / D_HID))
        x = jax.random.normal(k1, (B, S, D_IN), dtype=jnp.float32)
        in_weight = jax.random.uniform(k2, (D_HID, D_IN), dtype=jnp.float32, minval=-init_k, maxval=init_k)
        in_bias = jax.random.uniform(k3, (D_HID,), dtype=jnp.float32, minval=-init_k, maxval=init_k)
        out_weight = jax.random.uniform(k4, (D_HID, D_OUT), dtype=jnp.float32, minval=-init_k2, maxval=init_k2)
        return {'x': x, 'in_weight': in_weight, 'in_bias': in_bias, 'out_weight': out_weight}
    _L0_ffn_all = _L0_ffn_setup()
    _L0_ffn_in = {k: v for k, v in _L0_ffn_all.items() if k in ('in_weight', 'in_bias', 'out_weight')}
    del _L0_ffn_all

    def _L1_attn_setup():
        import jax, jax.numpy as jnp
        import numpy as np
        key = jax.random.key(seed)
        k1, k2, k3, k4, k5 = jax.random.split(key, 5)
        B, N, C = (16, 256, 192)
        x = jax.random.normal(k1, (B, N, C), dtype=jnp.float32)
        sc_token = jax.random.normal(k2, (1, 196, C), dtype=jnp.float32) * 0.02
        W_qkv = jax.random.normal(k3, (C, 3 * C), dtype=jnp.float32) * 0.02
        W_proj = jax.random.normal(k4, (C, C), dtype=jnp.float32) * 0.02
        b_proj = jax.random.normal(k5, (C,), dtype=jnp.float32) * 0.02
        return {'x': x, 'sc_token': sc_token, 'W_qkv': W_qkv, 'W_proj': W_proj, 'b_proj': b_proj}
    _L1_attn_all = _L1_attn_setup()
    _L1_attn_in = {k: v for k, v in _L1_attn_all.items() if k in ('sc_token', 'W_qkv', 'W_proj', 'b_proj')}
    del _L1_attn_all

    def _L1_ffn_setup():
        import jax, jax.numpy as jnp
        import numpy as np
        DIM = 192
        NUM_EXPERTS = 4
        NUM_HEADS = 12
        HEAD_DIM = DIM // NUM_HEADS
        MLP_HID = 4 * DIM
        FC1_OUT = MLP_HID + 3 * DIM
        FC2_IN = MLP_HID + DIM
        FC2_OUT = 2 * DIM
        CAP_FACTOR = 0.5
        LN_EPS = 1e-06
        key = jax.random.key(seed)
        ks = jax.random.split(key, 4)
        B, N = (8, 256)
        return {'x': jax.random.normal(ks[0], (B, N, DIM), jnp.float32), 'w_router': jax.random.normal(ks[1], (NUM_EXPERTS, DIM), jnp.float32) * 0.02, 'gamma1': jnp.ones((DIM,), jnp.float32), 'beta1': jnp.zeros((DIM,), jnp.float32), 'w1': jax.random.normal(ks[2], (FC1_OUT, DIM), jnp.float32) * 0.02, 'b1': jnp.zeros((FC1_OUT,), jnp.float32), 'w2': jax.random.normal(ks[3], (FC2_OUT, FC2_IN), jnp.float32) * 0.02, 'b2': jnp.zeros((FC2_OUT,), jnp.float32)}
    _L1_ffn_all = _L1_ffn_setup()
    _L1_ffn_in = {k: v for k, v in _L1_ffn_all.items() if k in ('w_router', 'gamma1', 'beta1', 'w1', 'b1', 'w2', 'b2')}
    del _L1_ffn_all
    return {'x': x, 'txt': txt, 'L0_tok_W': _L0_tok_in['W'], 'L0_attn_W_A': _L0_attn_in['W_A'], 'L0_attn_W_V': _L0_attn_in['W_V'], 'L0_attn_W_proj': _L0_attn_in['W_proj'], 'L0_attn_b_proj': _L0_attn_in['b_proj'], 'L0_ffn_in_weight': _L0_ffn_in['in_weight'], 'L0_ffn_in_bias': _L0_ffn_in['in_bias'], 'L0_ffn_out_weight': _L0_ffn_in['out_weight'], 'L1_attn_sc_token': _L1_attn_in['sc_token'], 'L1_attn_W_qkv': _L1_attn_in['W_qkv'], 'L1_attn_W_proj': _L1_attn_in['W_proj'], 'L1_attn_b_proj': _L1_attn_in['b_proj'], 'L1_ffn_w_router': _L1_ffn_in['w_router'], 'L1_ffn_gamma1': _L1_ffn_in['gamma1'], 'L1_ffn_beta1': _L1_ffn_in['beta1'], 'L1_ffn_w1': _L1_ffn_in['w1'], 'L1_ffn_b1': _L1_ffn_in['b1'], 'L1_ffn_w2': _L1_ffn_in['w2'], 'L1_ffn_b2': _L1_ffn_in['b2']}

def reference(x, txt, L0_tok_W, L0_attn_W_A, L0_attn_W_V, L0_attn_W_proj, L0_attn_b_proj, L0_ffn_in_weight, L0_ffn_in_bias, L0_ffn_out_weight, L1_attn_sc_token, L1_attn_W_qkv, L1_attn_W_proj, L1_attn_b_proj, L1_ffn_w_router, L1_ffn_gamma1, L1_ffn_beta1, L1_ffn_w1, L1_ffn_b1, L1_ffn_w2, L1_ffn_b2):
    import jax
    import jax.numpy as jnp

    def _L0_tok_ref(x, W):
        import jax, jax.numpy as jnp
        import numpy as np
        PATCH = 16
        LATENT = 192

        def _extract_patches(x, p):
            B, C, H, W_ = x.shape
            nh, nw = (H // p, W_ // p)
            patches = x.reshape(B, C, nh, p, nw, p).transpose(0, 1, 2, 4, 3, 5)
            return patches.reshape(B, nh * nw, C * p * p)
        patches = _extract_patches(x, PATCH)
        return jnp.einsum('bnk,ok->bno', patches, W)

    def _L0_attn_ref(x, W_A, W_V, W_proj, b_proj):
        import jax, jax.numpy as jnp
        import numpy as np
        DIM = 192
        NUM_HEADS = 12
        HEAD_DIM = DIM // NUM_HEADS
        B, N, C = x.shape
        h, hd = (NUM_HEADS, HEAD_DIM)
        z = jnp.einsum('bnc,ch->bhn', x, W_A)
        z_star = jax.nn.softmax(z, axis=-1)
        pos = jnp.arange(N)
        idx = (pos[None, :] - pos[:, None]) % N
        roll = z_star[:, :, idx] / N
        V = jnp.einsum('bnc,cd->bnd', x, W_V).reshape(B, N, h, hd).transpose(0, 2, 1, 3)
        out = jnp.einsum('bhij,bhjd->bhid', roll, V)
        out = out.transpose(0, 2, 1, 3).reshape(B, N, C)
        out = jnp.einsum('bnc,cd->bnd', out, W_proj) + b_proj
        return out

    def _L0_ffn_ref(x, in_weight, in_bias, out_weight):
        import jax, jax.numpy as jnp
        import numpy as np
        B, S, D_IN, D_HID, D_OUT = (32, 128, 192, 768, 192)
        lead = x.shape[:-1]
        xt = x.reshape(-1, in_weight.shape[1])
        h = jax.nn.gelu(jnp.einsum('td,hd->th', xt, in_weight) + in_bias, approximate=False)
        out = jnp.einsum('th,ho->to', h, out_weight)
        return out.reshape(*lead, out_weight.shape[1])

    def _L1_attn_ref(x, sc_token, W_qkv, W_proj, b_proj):
        import jax, jax.numpy as jnp
        import numpy as np
        B, N, C = x.shape
        H = 12
        Dh = C // H
        scale = Dh ** (-0.5)
        xt = jnp.concatenate([x, jnp.broadcast_to(sc_token, (B,) + sc_token.shape[1:])], axis=1)
        N1 = xt.shape[1]
        qkv = (xt @ W_qkv).reshape(B, N1, 3, H, Dh)
        q = qkv[:, :, 0].transpose(0, 2, 1, 3)
        k = qkv[:, :, 1].transpose(0, 2, 1, 3)
        v = qkv[:, :, 2].transpose(0, 2, 1, 3)
        attn = jax.nn.softmax(jnp.einsum('bhqd,bhkd->bhqk', q, k) * scale, axis=-1)
        out = jnp.einsum('bhqk,bhkd->bhqd', attn, v)
        out = out.transpose(0, 2, 1, 3).reshape(B, N1, C)
        out = out[:, :N, :]
        return out @ W_proj + b_proj

    def _L1_ffn_ref(x, w_router, gamma1, beta1, w1, b1, w2, b2):
        import jax, jax.numpy as jnp
        import numpy as np
        DIM = 192
        NUM_EXPERTS = 4
        NUM_HEADS = 12
        HEAD_DIM = DIM // NUM_HEADS
        MLP_HID = 4 * DIM
        FC1_OUT = MLP_HID + 3 * DIM
        FC2_IN = MLP_HID + DIM
        FC2_OUT = 2 * DIM
        CAP_FACTOR = 0.5
        LN_EPS = 1e-06
        B, N, C = x.shape
        E = NUM_EXPERTS
        cap = int(CAP_FACTOR * N)
        m = np.array([C // 2 ** (E - 1 - e) for e in range(E)])
        in_mask = (np.arange(C)[None, :] < m[:, None]).astype(np.float32)
        in_mask = jnp.asarray(in_mask)
        out_mask = jnp.concatenate([in_mask, in_mask], axis=-1)
        logits = jnp.einsum('bnc,ec->bne', x, w_router)
        probs = jax.nn.softmax(logits, axis=-1)
        gate, idx = jax.lax.top_k(jnp.swapaxes(probs, 1, 2), cap)
        dispatch = jax.nn.one_hot(idx, N, dtype=x.dtype)
        combine = dispatch * gate[..., None]
        mu = jnp.mean(x, -1, keepdims=True)
        var = jnp.var(x, -1, keepdims=True)
        y = (x - mu) * jax.lax.rsqrt(var + LN_EPS) * gamma1 + beta1
        xg = jnp.einsum('becn,bnd->becd', dispatch, y)
        xg = xg * in_mask[None, :, None, :]
        h = jnp.einsum('becd,fd->becf', xg, w1) + b1
        h = jnp.einsum('becn,becf->bnf', dispatch, h)
        x_mlp, x_qkv = (h[..., :MLP_HID], h[..., MLP_HID:])
        qkv = x_qkv.reshape(B, N, 3, NUM_HEADS, HEAD_DIM).transpose(2, 0, 3, 1, 4)
        q, k, v = (qkv[0], qkv[1], qkv[2])
        scale = HEAD_DIM ** (-0.5)
        attn = jax.nn.softmax(jnp.einsum('bhqd,bhkd->bhqk', q, k) * scale, axis=-1)
        x_attn = jnp.einsum('bhqk,bhkd->bhqd', attn, v)
        x_attn = x_attn.transpose(0, 2, 1, 3).reshape(B, N, C)
        x_mlp = jax.nn.gelu(x_mlp, approximate=False)
        y2 = jnp.concatenate([x_mlp, x_attn], axis=-1)
        yg = jnp.einsum('becn,bnf->becf', dispatch, y2)
        o = jnp.einsum('becf,of->beco', yg, w2) + b2
        o = o * out_mask[None, :, None, :]
        z = jnp.einsum('becn,beco->bno', combine, o)
        x_mlp2, x_attn2 = (z[..., :C], z[..., C:])
        return x + x_mlp2 + x_attn2
    h = _L0_tok_ref(x, L0_tok_W)
    h = jnp.concatenate([h, txt], axis=1)
    h = h + _L0_attn_ref(_layernorm(h, axis=-1), L0_attn_W_A, L0_attn_W_V, L0_attn_W_proj, L0_attn_b_proj)
    h = h + _L0_ffn_ref(_layernorm(h, axis=-1), L0_ffn_in_weight, L0_ffn_in_bias, L0_ffn_out_weight)
    h = h + _L1_attn_ref(_layernorm(h, axis=-1), L1_attn_sc_token, L1_attn_W_qkv, L1_attn_W_proj, L1_attn_b_proj)
    h = h + _L1_ffn_ref(_layernorm(h, axis=-1), L1_ffn_w_router, L1_ffn_gamma1, L1_ffn_beta1, L1_ffn_w1, L1_ffn_b1, L1_ffn_w2, L1_ffn_b2)
    return h

_drawn_inputs = setup_inputs


def setup_inputs(seed=0):
    import zlib

    import numpy as np

    out = dict(_drawn_inputs(seed))
    spreads = {'L1_ffn_gamma1': (1.0, 0.6),
     'L1_ffn_beta1': (0.0, 0.8),
     'L1_ffn_b1': (0.0, 0.1),
     'L1_ffn_b2': (0.0, 0.1)}
    factors = {'L0_attn_W_A': 26.422,
     'L0_attn_W_V': 26.828,
     'L0_attn_W_proj': 25.798,
     'L1_attn_sc_token': 200.0}
    for name, (base, spread) in spreads.items():
        noise = np.random.default_rng([zlib.crc32(name.encode()), seed]).standard_normal(out[name].shape)
        drawn = base * np.exp(spread * noise) if base else spread * noise
        out[name] = jnp.asarray(drawn.astype(out[name].dtype))
    for name, factor in factors.items():
        out[name] = (out[name] * factor).astype(out[name].dtype)
    return out
```

```python
import numpy as np
import concourse.bass as bass
from concourse import mybir
from contextlib import ExitStack

B = 16
IMG, TXT, SC = 196, 128, 196
N = IMG + TXT
C = 192
P, T = 108, 3
KC = 96
H, D = 12, 16
NK1 = N + SC
TK1, KT1 = 104, 5
TK2, KT2 = P, T
FH = 768
FT = FH // 128
E, CAP = 4, N // 2
PAD = 8 * ((CAP + 7) // 8) - CAP
ROUNDS = (CAP + PAD) // 8
NF = N // 2 + 1
FW = 82
SCALE = float(D) ** -0.5
Q_PARTS = (0, 0, 0, 1, 1, 2)
K_PARTS = (0, 1, 2, 0, 1, 0)
GROUPS = 3


class Signal:

    def __init__(self, sem, per, primed=1):
        self.sem, self.per, self.primed = sem, per, primed

    def at(self, i, n):
        return (i + self.primed) * self.per + n


def build(nc, A):
    fp32, bf16, i32 = mybir.dt.float32, mybir.dt.bfloat16, mybir.dt.int32
    ALU, ACT, AX = mybir.AluOpType, mybir.ActivationFunctionType, mybir.AxisListType
    ctx = ExitStack()
    with ctx:
        def sb(name, shape, dt=fp32):
            return ctx.enter_context(nc.sbuf_tensor(name, shape, dt))

        primed = []

        def signal(name, per=1, prime=1):
            s = Signal(ctx.enter_context(nc.semaphore(name)), per, prime)
            if per and prime:
                primed.append(s)
            return s

        w_tok = sb("w_tok", [128, 2, C])
        w_a = sb("w_a", [KC, 2, H])
        w_v0 = sb("w_v0", [KC, 2, C])
        w_p0 = sb("w_p0", [KC, 2, C])
        b_p0 = sb("b_p0", [P, C])
        w_in = sb("w_in", [KC, 2, FH])
        b_in = sb("b_in", [128, FT])
        w_out = sb("w_out", [128, FT, C])
        w_qkv = sb("w_qkv", [KC, 2, 3 * C])
        w_p1 = sb("w_p1", [128, GROUPS, C])
        b_p1 = sb("b_p1", [P, C])
        w_r = sb("w_r", [KC, 2, E])
        gamma = sb("gamma", [KC, 2])
        beta = sb("beta", [KC, 2])
        w_1 = sb("w_1", [KC, 2, FH + 3 * C])
        b_1 = sb("b_1", [E, FH + 3 * C])
        w_2 = sb("w_2", [128, 2, FT, C])
        w_2a = sb("w_2a", [128, 2, GROUPS, C])
        b_2 = sb("b_2", [P, 2, C])
        ident = sb("ident", [128, 128])
        identb = sb("identb", [128, 128], bf16)
        dft = sb("dft", [P, T, 2, 2, FW])
        idft = sb("idft", [FW, 2, 2, N])
        spread = sb("spread", [128, 128])
        emask = sb("emask", [E, C])

        pT = sb("pT", [128, 2, IMG])
        hin = sb("hin", [P, T, C])
        hb = sb("hb", [P, T, C])
        h = sb("h", [P, T, C])
        xn = sb("xn", [P, T, C])
        xn5 = sb("xn5", [P, T, C])
        st = sb("st", [P, T, 6])
        mv = sb("mv", [P, T, 2])
        var = sb("var", [P, T])
        rs = sb("rs", [P, T])
        nt = sb("nt", [P, T])
        xT = sb("xT", [KC, 2, N])
        xS = sb("xS", [KC, 2, NK1])
        nmz = sb("nmz", [H, 1])
        zsum = sb("zsum", [H, 1])
        zrec = sb("zrec", [H, 1])
        zexp = sb("zexp", [H, N])
        vz = sb("vz", [P, T, C + H])
        zf = sb("zf", [FW, 2, 2, H])
        ta = sb("ta", [FW, 2, C])
        tb = sb("tb", [FW, 2, C])
        of = sb("of", [FW, 2, 2, C])
        aT = sb("aT", [KC, 2, N])
        g = sb("g", [128, FT, N])
        piece = sb("piece", [KC, 4, 3, N], bf16)
        rest = sb("rest", [KC, 4, N])
        qpack = sb("qpack", [99, H, N], bf16)
        kpack = sb("kpack", [99, H, NK1], bf16)
        v1 = sb("v1", [TK1, KT1, H, 32])
        v2 = sb("v2", [TK2, KT2, H, 32])
        mxh = sb("mxh", [P, H, T, 2])
        mx = sb("mx", [P, T, H])
        mr = sb("mr", [P, T, H])
        mp = sb("mp", [P, T, 3, H], bf16)
        mT = sb("mT", [3 * H, N], bf16)
        NP = 8
        prob = sb("prob", [128, NP, N])
        av = sb("av", [128, GROUPS, N])
        rc = sb("rc", [128, N])
        lg = sb("lg", [P, T, E])
        lmx = sb("lmx", [P, T])
        pr = sb("pr", [P, T, E])
        prT = sb("prT", [E, N])
        work = sb("work", [E, N + PAD])
        top8 = sb("top8", [E, 8])
        sel = sb("sel", [E, N])
        gate = sb("gate", [E, N])
        yT = sb("yT", [KC, 2, N])
        gm = sb("gm", [P, T, C])
        fin = sb("fin", [P, T, C])
        hx = sb("hx", [P, T, C])

        lin = ctx.enter_context(nc.psum_tensor("lin", [128, 2, 512], fp32))
        mps = ctx.enter_context(nc.psum_tensor("mps", [128, 2, 512], fp32))
        sps = ctx.enter_context(nc.psum_tensor("sps", [128, 3, 512], fp32))
        aps = ctx.enter_context(nc.psum_tensor("aps", [128, 512], fp32))

        scr = nc.dram_tensor("scr", (2, 3, C, N), bf16, kind="Internal").ap()

        USES = (["act"]
                + ["act"] * 2
                + ["dve"]
                + ["act"] * 2
                + ["dve"]
                + ["dve"] * 2
                + ["act"] * 2
                + ["dve"] * 2
                + ["act"] * 2
                + ["act"] * 6
                + ["dve"] * 2
                + ["act"] * 2
                + ["dve"] * 4
                + ["act"] * 2
                + ["act"]
                + ["dve"] * 3
                + ["dve"] * 2
                + ["act"] * 2
                + ["dve"] * 2
                + ["act"] * 2
                + ["dve"] * 2
                + ["act"] * 6
                + ["dve"] * 4
                + ["act"] * 2
                + ["act"]
                + ["dve"] * 3
                + ["act"] * 2
                + ["dve"] * 2)
        NU = len(USES)
        lin_full = signal("lin_full", NU)
        lin_free = {"act": signal("lin_free_act", USES.count("act")),
                    "dve": signal("lin_free_dve", USES.count("dve"))}

        def order(u):
            return USES[:u + 1].count(USES[u])

        MU1, MU2 = 2 * H * T, H * T
        MU = MU1 + MU2
        SU1 = H * KT1
        SU = H * (KT1 + KT2)
        loads = signal("loads", 0)
        sc_in = signal("sc_in", 0)
        setup_dve = signal("setup_dve", 0)
        setup_pe = signal("setup_pe", 0)
        setup_act = signal("setup_act", 0)
        setup_pool = signal("setup_pool", 0)
        sc_first = signal("sc_first", 0)
        sc_rest = signal("sc_rest", 0)
        sc_mid = signal("sc_mid", 0)
        sc_pieces = signal("sc_pieces", 0)
        sc_scr = signal("sc_scr", 0)
        sc_pack = signal("sc_pack", 0)
        x_in = signal("x_in", 48, prime=0)
        tok_read = signal("tok_read")
        hin_read = signal("hin_read")
        hb_ready = signal("hb_ready", 2)
        hb_in = signal("hb_in", 1)
        ln_done = signal("ln_done", 5)
        xT_ready = signal("xT_ready", 10)
        nmz_ready = signal("nmz_ready")
        zexp_ready = signal("zexp_ready")
        zs_ready = signal("zs_ready")
        v0_ready = signal("v0_ready")
        vz_ready = signal("vz_ready")
        of_ready = signal("of_ready")
        aT_ready = signal("aT_ready", 2)
        g_ready = signal("g_ready", 12)
        res_done = signal("res_done", 2)
        split1 = signal("split1", 8)
        split2 = signal("split2", 8)
        split3 = signal("split3", 8)
        scr_in = signal("scr_in", 128)
        pack_in = signal("pack_in", 2 * 12 * 16)
        v_ready = signal("v_ready", 4)
        max_full = signal("max_full", MU)
        max_free = signal("max_free", MU)
        mp_ready = signal("mp_ready", 2)
        mrow_in = signal("mrow_in", 2 * 3 * 16)
        s_full = signal("s_full", SU)
        p_ready = signal("p_ready", SU)
        p_used = signal("p_used", SU)
        a_copied = signal("a_copied", 2 * GROUPS)
        av_ready = signal("av_ready", 2 * GROUPS)
        lg_ready = signal("lg_ready")
        pe_ready = signal("pe_ready")
        pr_ready = signal("pr_ready")
        sel_ready = signal("sel_ready")
        yT_ready = signal("yT_ready")
        gm_ready = signal("gm_ready", 2)
        hx_ready = signal("hx_ready")
        batch_done = signal("batch_done")
        out_sem = signal("out_sem", 16)
        dve_link = signal("dve_link", 0)
        gate_pe = signal("gate_pe", 0)
        gate_pool = signal("gate_pool", 0)

        block = ctx.enter_context(nc.Block())

        LOADS = [
            (w_tok, A["w_tok"]), (w_a, A["w_a"]), (w_v0, A["w_v0"]), (w_p0, A["w_p0"]),
            (w_in, A["w_in"]), (b_in, A["b_in"]), (w_out, A["w_out"]), (w_qkv, A["w_qkv"]),
            (w_r, A["w_r"]), (gamma, A["gamma"]), (beta, A["beta"]), (w_1, A["w_1"]),
            (w_2, A["w_2"]), (ident, A["ident"]), (dft, A["dft"]), (idft, A["idft"]),
            (spread, A["spread"]), (emask, A["emask"])]
        NLOAD = len(LOADS) + 3 * H + E + 3 + 1

        def tiles2(bank, rows, nt):
            return lin[0:rows, bank, :].rearrange("p (t c) -> p t c", t=2)[:, 0:nt, 0:C]

        @block.sync
        def _(sp):
            for s in primed:
                sp.sem_inc(s.sem, s.per)
            for dst, src in LOADS:
                sp.dma_start(dst.ap(), src).then_inc(loads.sem, 16)
            sp.wait_ge(setup_pool.sem, 2)
            for hd in range(H):
                r = 32 * (hd % 4)
                sp.dma_start(w_p1[r:r + D, hd // 4, :], A["w_p1"][hd * D:(hd + 1) * D, :]).then_inc(loads.sem, 16)
                for s in range(2):
                    sp.dma_start(w_2a[r:r + D, s, hd // 4, :],
                                 A["w_2a"][s, hd * D:(hd + 1) * D, :]).then_inc(loads.sem, 16)
            for e in range(E):
                sp.dma_start(b_1[e:e + 1, :], A["b_1"]).then_inc(loads.sem, 16)
            sp.dma_start(b_p0[:, :], A["b_p0"].partition_broadcast(P)).then_inc(loads.sem, 16)
            sp.dma_start(b_p1[:, :], A["b_p1"].partition_broadcast(P)).then_inc(loads.sem, 16)
            sp.dma_start(b_2[:, :, :], A["b_2"].partition_broadcast(P)).then_inc(loads.sem, 16)
            sp.dma_start(xS[:, :, N:NK1], A["sc"]).then_inc(loads.sem, 16)
            sp.wait_ge(sc_pieces.sem, 2)
            for m in range(2):
                sp.dma_start(scr[1, :, m * KC:(m + 1) * KC, 0:SC].rearrange("s p n -> p s n"),
                             piece[:, 2 + m, :, 0:SC]).then_inc(sc_scr.sem, 16)
            sp.wait_ge(sc_scr.sem, 32)
            for r, s in enumerate(K_PARTS):
                sp.dma_start(kpack[r * D:(r + 1) * D, :, N:NK1],
                             scr[1, s, :, 0:SC].rearrange("(h d) n -> d h n", d=D)).then_inc(sc_pack.sem, 16)
            sp.wait_ge(sc_pack.sem, 16 * 6)
            with sp.Fori(0, B) as i:
                for a in range(2):
                    for m in range(4):
                        sp.wait_ge(split3.sem, split3.at(i, 4 * a + m + 1))
                        sp.dma_start(scr[m // 2, :, (m % 2) * KC:(m % 2 + 1) * KC, :].rearrange("s p n -> p s n"),
                                     piece[:, m, :, :]).then_inc(scr_in.sem, 16)
                    sp.wait_ge(scr_in.sem, scr_in.at(i, 64 * (a + 1)))
                    if a == 1:
                        sp.wait_ge(p_ready.sem, p_ready.at(i, SU1))
                    for r in range(6):
                        sp.dma_start(qpack[r * D:(r + 1) * D, :, :],
                                     scr[0, Q_PARTS[r], :, :].rearrange("(h d) n -> d h n", d=D)).then_inc(pack_in.sem, 16)
                        sp.dma_start(kpack[r * D:(r + 1) * D, :, 0:N],
                                     scr[1, K_PARTS[r], :, :].rearrange("(h d) n -> d h n", d=D)).then_inc(pack_in.sem, 16)
                    sp.wait_ge(lin_free["act"].sem, lin_free["act"].at(i, order((31, 57)[a])))
                    for s in range(3):
                        sp.dma_start(qpack[6 * D + s:6 * D + s + 1, :, :], mT[s * H:(s + 1) * H, :]).then_inc(mrow_in.sem, 16)
                sp.wait_ge(batch_done.sem, batch_done.at(i, 1))
                sp.dma_start(A["out"][i].rearrange("(t p) c -> p t c", p=P), fin[:, :, :]).then_inc(out_sem.sem, 16)
            sp.wait_ge(out_sem.sem, out_sem.at(B, 0))

        @block.gpsimd
        def _(pool):
            nc.gpsimd.memset(w_p1[:, :, :], 0.0).then_inc(setup_pool.sem, 1)
            nc.gpsimd.memset(w_2a[:, :, :, :], 0.0).then_inc(setup_pool.sem, 1)
            nc.gpsimd.memset(v1[:, :, :, :], 0.0).then_inc(setup_pool.sem, 1)
            nc.gpsimd.memset(v2[:, :, :, :], 0.0).then_inc(setup_pool.sem, 1)
            pool.wait_ge(setup_pool.sem, 4)
            nc.gpsimd.memset(v1[:, :, :, D:D + 1], 1.0).then_inc(setup_pool.sem, 1)
            nc.gpsimd.memset(v2[:, :, :, D:D + 1], 1.0).then_inc(setup_pool.sem, 1)
            pool.wait_ge(setup_pool.sem, 6)
            nc.gpsimd.memset(kpack[6 * D:6 * D + 3, :, :], 1.0).then_inc(setup_pool.sem, 1)

            def load_x(j):
                pool.dma_start(pT[:, :, :], A["x"][j]).then_inc(x_in.sem, 16)
                pool.dma_start(hin[IMG - P:P, 1, :], A["txt"][j, 0:2 * P - IMG, :]).then_inc(x_in.sem, 16)
                pool.dma_start(hin[:, 2, :], A["txt"][j, 2 * P - IMG:TXT, :]).then_inc(x_in.sem, 16)

            for m in range(2, 4):
                pool.wait_ge(sc_rest.sem, m - 1)
                nc.gpsimd.tensor_copy(piece[:, m, 1, 0:SC], rest[:, m, 0:SC]).then_inc(sc_mid.sem, 1)
                pool.wait_ge(sc_mid.sem, m - 1)
                nc.gpsimd.tensor_tensor(piece[:, m, 2, 0:SC], rest[:, m, 0:SC], piece[:, m, 1, 0:SC],
                                        ALU.subtract).then_inc(sc_pieces.sem, 1)
            pool.wait_ge(loads.sem, 16 * NLOAD)
            load_x(0)
            with pool.Fori(0, B) as i:
                pool.wait_ge(x_in.sem, x_in.at(i, 48))
                pool.wait_ge(lin_free["act"].sem, lin_free["act"].at(i, 1))
                for t in range(T):
                    last = nc.gpsimd.tensor_tensor(hb[:, t, :], hin[:, t, :], b_p0[:, :], ALU.add)
                last.then_inc(hb_ready.sem, 1)
                pool.wait_ge(ln_done.sem, ln_done.at(i, 1))
                pool.wait_ge(hb_ready.sem, hb_ready.at(i, 1))
                load_x((i + 1) % B)
                for a in range(2):
                    if a == 0:
                        pool.wait_ge(res_done.sem, res_done.at(i, 2))
                        for t in range(T):
                            last = nc.gpsimd.tensor_tensor(hb[:, t, :], h[:, t, :], b_p1[:, :], ALU.add)
                        last.then_inc(hb_ready.sem, 1)
                    for m in range(4):
                        pool.wait_ge(lin_free["dve"].sem, lin_free["dve"].at(i, order((25, 51)[a] + m)))
                        pool.wait_ge(scr_in.sem, scr_in.at(i, 64 * a))
                        pool.sem_inc(gate_pool.sem)
                        nc.gpsimd.tensor_copy(piece[:, m, 1, :], rest[:, m, :]).then_inc(split2.sem, 1)
                        pool.wait_ge(split2.sem, split2.at(i, 4 * a + m + 1))
                        nc.gpsimd.tensor_tensor(piece[:, m, 2, :], rest[:, m, :], piece[:, m, 1, :],
                                                ALU.subtract).then_inc(split3.sem, 1)
                pool.wait_ge(ln_done.sem, ln_done.at(i, 4))
                nc.gpsimd.tensor_tensor(hx[:, :, :], h[:, :, :], xn[:, :, :], ALU.add).then_inc(hx_ready.sem, 1)
            pool.wait_ge(x_in.sem, x_in.at(B, 48))

        @block.scalar
        def _(act):
            act.wait_ge(loads.sem, 16 * NLOAD)

            def take(i, u):
                act.wait_ge(lin_full.sem, lin_full.at(i, u + 1))

            def free():
                return lin_free["act"].sem

            for m in range(2):
                act.wait_ge(setup_pe.sem, m + 1)
                nc.scalar.copy(piece[:, 2 + m, 0, 0:SC], lin[0:KC, m, 0:SC]).then_inc(sc_first.sem, 1)
            act.wait_ge(setup_pe.sem, 3)
            act.wait_ge(setup_pool.sem, 7)
            nc.scalar.copy(v1[:, KT1 - 1, :, 0:D],
                           mps[0:TK1, 0, 0:C].rearrange("p (h d) -> p h d", d=D)).then_inc(setup_act.sem, 1)

            with act.Fori(0, B) as i:
                def copy_xT(u, dst):
                    for k in range(2):
                        take(i, u + k)
                        nc.scalar.copy(dst[:, k, 0:N], lin[0:KC, (u + k) % 2, 0:N]).then_inc(free(), 1)

                take(i, 0)
                act.wait_ge(batch_done.sem, batch_done.at(i, 0))
                act.wait_ge(hx_ready.sem, hx_ready.at(i, 0))
                nc.scalar.copy(hin[:, 0, :], lin[0:P, 0, 0:C])
                act.wait_ge(x_in.sem, x_in.at(i, 48))
                nc.scalar.copy(hin[0:IMG - P, 1, :], lin[0:IMG - P, 0, 256:256 + C]).then_inc(free(), 1)
                copy_xT(1, xT)
                act.wait_ge(nmz_ready.sem, nmz_ready.at(i, 1))
                nc.scalar.activation(zexp[:, :], lin[0:H, 1, 0:N], ACT.Exp, bias=nmz[:, 0:1],
                                     accum_out=zsum[:, 0:1]).then_inc(zexp_ready.sem, 1)
                take(i, 4)
                nc.scalar.copy(vz[:, 0:2, 0:C], tiles2(0, P, 2)).then_inc(free(), 1)
                take(i, 5)
                nc.scalar.copy(vz[:, 2:3, 0:C], tiles2(1, P, 1)).then_inc(free(), 1)
                for k in range(2):
                    take(i, 9 + k)
                    nc.scalar.copy(aT[:, k, :], lin[0:KC, (9 + k) % 2, 0:N]).then_inc(free(), 1)
                copy_xT(13, xT)
                for f in range(FT):
                    take(i, 15 + f)
                    nc.scalar.activation(g[:, f, :], lin[:, (15 + f) % 2, 0:N], ACT.Gelu,
                                         bias=b_in[:, f:f + 1]).then_inc(free(), 1)
                copy_xT(23, xS)

                def first_parts(a, u):
                    for m in range(4):
                        take(i, u + m)
                        act.wait_ge(scr_in.sem, scr_in.at(i, 64 * a))
                        nc.scalar.copy(piece[:, m, 0, :], lin[0:KC, (u + m) % 2, 0:N]).then_inc(split1.sem, 1)

                def values(u, rows, nt, dst):
                    for k in range(2):
                        m = min(2, nt - 2 * k)
                        take(i, u + k)
                        src = lin[0:rows, (u + k) % 2, :].rearrange("p (t c) -> p t c", t=2)
                        for s in range(m):
                            last = nc.scalar.copy(dst[:, 2 * k + s, :, 0:D],
                                                  src[:, s, 0:C].rearrange("p (h d) -> p h d", d=D))
                        last.then_inc(free(), 1)

                def exps(base, kt, rows):
                    for n in range(base, base + H * kt):
                        act.wait_ge(s_full.sem, s_full.at(i, n + 1))
                        if n >= NP:
                            act.wait_ge(p_used.sem, p_used.at(i, n - NP + 1))
                        nc.scalar.activation(prob[0:rows, n % NP, :], sps[0:rows, n % 3, 0:N], ACT.Exp,
                                             scale=SCALE).then_inc(p_ready.sem, 1)

                first_parts(0, 25)
                values(29, TK1, 4, v1)
                take(i, 31)
                nc.scalar.copy(mT[:, :], lin[0:3 * H, 1, 0:N // 2].bitcast(bf16)).then_inc(free(), 1)
                exps(0, KT1, TK1)
                copy_xT(37, xT)
                act.wait_ge(lg_ready.sem, lg_ready.at(i, 1))
                nc.scalar.activation(pr[:, :, :], lg[:, :, :], ACT.Exp).then_inc(pe_ready.sem, 1)
                copy_xT(41, xT)
                for f in range(FT):
                    take(i, 45 + f)
                    nc.scalar.activation(g[:, f, :], lin[:, (45 + f) % 2, 0:N], ACT.Gelu).then_inc(free(), 1)
                first_parts(1, 51)
                values(55, TK2, 3, v2)
                take(i, 57)
                act.wait_ge(mrow_in.sem, mrow_in.at(i, 48))
                nc.scalar.copy(mT[:, :], lin[0:3 * H, 1, 0:N // 2].bitcast(bf16)).then_inc(free(), 1)
                exps(SU1, KT2, TK2)
                take(i, 61)
                nc.scalar.copy(gm[:, 0:2, :], tiles2(1, P, 2)).then_inc(free(), 1)
                take(i, 62)
                nc.scalar.copy(gm[:, 2:3, :], tiles2(0, P, 1)).then_inc(free(), 1)

        @block.vector
        def _(dve):
            dve.wait_ge(loads.sem, 16 * NLOAD)
            nc.vector.tensor_copy(identb[:, :], ident[:, :]).then_inc(setup_dve.sem, 1)
            nc.vector.tensor_tensor(w_2[:, 0], w_2[:, 0], w_2[:, 1], ALU.add).then_inc(setup_dve.sem, 1)
            nc.vector.tensor_tensor(w_2a[:, 0], w_2a[:, 0], w_2a[:, 1], ALU.add).then_inc(setup_dve.sem, 1)
            nc.vector.tensor_tensor(b_2[:, 0], b_2[:, 0], b_2[:, 1], ALU.add).then_inc(setup_dve.sem, 1)
            for m in range(2):
                dve.wait_ge(sc_first.sem, m + 1)
                nc.vector.tensor_tensor(rest[:, 2 + m, 0:SC], lin[0:KC, m, 0:SC], piece[:, 2 + m, 0, 0:SC],
                                        ALU.subtract).then_inc(sc_rest.sem, 1)
            dve.wait_ge(setup_dve.sem, 4)

            with dve.Fori(0, B) as i:
                links = [0]
                dve.sem_clear(dve_link.sem)

                def link(ins):
                    links[0] += 1
                    ins.then_inc(dve_link.sem, 1)
                    dve.wait_ge(dve_link.sem, links[0])

                def take(u):
                    dve.wait_ge(lin_full.sem, lin_full.at(i, u + 1))

                def free():
                    return lin_free["dve"].sem

                def layernorm(src, dst, eps):
                    for t in range(T):
                        last = nc.vector.bn_stats(st[:, t, :], src[:, t, :])
                    link(last)
                    for t in range(T):
                        last = nc.vector.bn_aggr(mv[:, t, :], st[:, t, :])
                    link(last)
                    link(nc.vector.tensor_scalar(var[:, :], mv[:, :, 1], eps, None, ALU.add))
                    link(nc.vector.tensor_scalar(rs[:, :].bitcast(i32), var[:, :].bitcast(i32), -0.5, 1597463007.0,
                                                 ALU.mult, ALU.add))
                    for _ in range(4):
                        link(nc.vector.tensor_tensor(nt[:, :], rs[:, :], rs[:, :], ALU.mult))
                        link(nc.vector.tensor_tensor(nt[:, :], nt[:, :], var[:, :], ALU.mult))
                        link(nc.vector.tensor_scalar(nt[:, :], nt[:, :], -0.5, 1.5, ALU.mult, ALU.add))
                        link(nc.vector.tensor_tensor(rs[:, :], rs[:, :], nt[:, :], ALU.mult))
                    for t in range(T):
                        last = nc.vector.tensor_scalar(dst[:, t, :], src[:, t, :], mv[:, t, 0:1], rs[:, t:t + 1],
                                                       ALU.subtract, ALU.mult)
                    last.then_inc(ln_done.sem, 1)

                def residual(u, k):
                    take(u)
                    nc.vector.tensor_tensor(h[:, 0:2, :], tiles2(u % 2, P, 2), (hb if k != 1 else h)[:, 0:2, :],
                                            ALU.add).then_inc(free(), 1)
                    take(u + 1)
                    nc.vector.tensor_tensor(h[:, 2:3, :], tiles2((u + 1) % 2, P, 1), (hb if k != 1 else h)[:, 2:3, :],
                                            ALU.add).then_inc(free(), 1)
                    dve.wait_ge(free(), lin_free["dve"].at(i, order(u + 1)))
                    return

                dve.wait_ge(lin_free["act"].sem, lin_free["act"].at(i, 1))
                dve.wait_ge(hx_ready.sem, hx_ready.at(i, 0))
                layernorm(hin, xn, 1e-5)
                take(3)
                nc.vector.tensor_reduce(nmz[:, 0:1], lin[0:H, 1, 0:N], AX.X, ALU.max, negate=True).then_inc(nmz_ready.sem, 1)
                dve.wait_ge(zexp_ready.sem, zexp_ready.at(i, 1))
                nc.vector.reciprocal(zrec[:, :], zsum[:, :]).then_inc(free(), 1)
                dve.wait_ge(free(), lin_free["dve"].at(i, 1))
                nc.vector.tensor_scalar(zexp[:, :], zexp[:, :], zrec[:, 0:1], 1.0 / N, ALU.mult,
                                        ALU.mult).then_inc(zs_ready.sem, 1)
                take(6)
                nc.vector.tensor_copy(vz[:, :, C:C + H],
                                      lin[0:P, 0, 0:T * H].rearrange("p (t h) -> p t h", t=T)).then_inc(free(), 1)
                vr, vi = (lin[0:FW, s, :].rearrange("p (f c) -> p f c", f=2) for s in (1, 0))
                take(7)
                link(nc.vector.tensor_copy(zf[:, 0, :, :], vr[:, :, C:C + H]))
                take(8)
                link(nc.vector.tensor_copy(zf[:, 1, :, :], vi[:, :, C:C + H]))

                def times(dst, v, part):
                    for f in range(2):
                        last = nc.vector.tensor_tensor(
                            dst[:, f, :].rearrange("p (h d) -> p h d", d=D),
                            v[:, f, 0:C].rearrange("p (h d) -> p h d", d=D),
                            zf[:, part, f, :].rearrange("p (h a) -> p h a", a=1).broadcast_to([FW, H, D]), ALU.mult)
                    return last

                times(ta, vr, 0)
                link(times(tb, vi, 1))
                link(nc.vector.tensor_tensor(of[:, 0], ta[:, :, :], tb[:, :, :], ALU.add))
                times(ta, vi, 0)
                link(times(tb, vr, 1))
                nc.vector.tensor_tensor(of[:, 1], ta[:, :, :], tb[:, :, :], ALU.subtract).then_inc(of_ready.sem, 1)
                dve.wait_ge(of_ready.sem, of_ready.at(i, 1))
                nc.vector.tensor_copy(zf[:, 0, 0, 0:1], zf[:, 0, 0, 0:1]).then_inc(free(), 2)
                dve.wait_ge(hb_ready.sem, hb_ready.at(i, 1))
                residual(11, 0)
                layernorm(h, xn, 1e-5)
                residual(21, 1)
                nc.vector.tensor_copy(zf[:, 0, 0, 0:1], zf[:, 0, 0, 0:1]).then_inc(res_done.sem, 2)
                layernorm(h, xn, 1e-5)

                def rests(a, u):
                    for m in range(4):
                        take(u + m)
                        dve.wait_ge(split1.sem, split1.at(i, 4 * a + m + 1))
                        if a == 1:
                            dve.wait_ge(split3.sem, split3.at(i, 4))
                        nc.vector.tensor_tensor(rest[:, m, :], lin[0:KC, (u + m) % 2, 0:N], piece[:, m, 0, :],
                                                ALU.subtract).then_inc(free(), 1)

                def maxima(a, base, halves, w):
                    n = base
                    for hd in range(H):
                        for t in range(T):
                            for s in range(halves):
                                dve.wait_ge(max_full.sem, max_full.at(i, n + 1))
                                last = nc.vector.tensor_reduce(mxh[:, hd, t, s:s + 1], mps[0:P, n % 2, 0:w],
                                                               AX.X, ALU.max, negate=halves == 1)
                                last.then_inc(max_free.sem, 1)
                                n += 1
                    dve.wait_ge(max_free.sem, max_free.at(i, n))
                    src = mxh[:, :, :, 0].rearrange("p h t -> p t h")
                    if halves == 2:
                        link(nc.vector.tensor_tensor(mr[:, :, :], src, mxh[:, :, :, 1].rearrange("p h t -> p t h"), ALU.max))
                        link(nc.vector.tensor_scalar(mx[:, :, :], mr[:, :, :], -1.0, None, ALU.mult))
                    else:
                        link(nc.vector.tensor_copy(mx[:, :, :], src))
                    link(nc.vector.tensor_copy(mp[:, :, 0, :], mx[:, :, :]))
                    link(nc.vector.tensor_tensor(mr[:, :, :], mx[:, :, :], mp[:, :, 0, :], ALU.subtract))
                    link(nc.vector.tensor_copy(mp[:, :, 1, :], mr[:, :, :]))
                    nc.vector.tensor_tensor(mp[:, :, 2, :], mr[:, :, :], mp[:, :, 1, :], ALU.subtract).then_inc(mp_ready.sem, 1)

                def normalise(a, u):
                    for q in range(GROUPS):
                        take(u + q)
                        if q:
                            dve.wait_ge(av_ready.sem, av_ready.at(i, GROUPS * a + q))
                        nc.vector.reciprocal(rc[:, :], lin[:, (u + q) % 2, 0:N]).then_inc(free(), 1)
                        dve.wait_ge(free(), lin_free["dve"].at(i, order(u + q)))
                        nc.vector.tensor_tensor(av[:, q, :], av[:, q, :], rc[:, :], ALU.mult).then_inc(av_ready.sem, 1)

                def sums(a):
                    for q in range(GROUPS):
                        dve.wait_ge(p_used.sem, p_used.at(i, a * SU1 + (q + 1) * 4 * (KT2 if a else KT1)))
                        nc.vector.tensor_copy(av[:, q, :], aps[:, 0:N]).then_inc(a_copied.sem, 1)

                rests(0, 25)
                maxima(0, 0, 2, NK1 // 2)
                sums(0)
                normalise(0, 32)
                dve.wait_ge(hb_ready.sem, hb_ready.at(i, 2))
                residual(35, 2)
                layernorm(h, xn, 1e-5)
                dve.wait_ge(ln_done.sem, ln_done.at(i, 4))
                layernorm(xn, xn5, 1e-6)
                take(39)
                lgp = lin[0:P, 1, 0:T * E].rearrange("p (t e) -> p t e", t=T)
                link(nc.vector.tensor_reduce(lmx[:, :], lgp, AX.X, ALU.max))
                for t in range(T):
                    last = nc.vector.tensor_scalar(lg[:, t, :], lgp[:, t, :], lmx[:, t:t + 1], None, ALU.subtract)
                last.then_inc(free(), 1)
                dve.wait_ge(free(), lin_free["dve"].at(i, order(39)))
                nc.vector.tensor_copy(nt[:, :], nt[:, :]).then_inc(lg_ready.sem, 1)
                dve.wait_ge(pe_ready.sem, pe_ready.at(i, 1))
                link(nc.vector.tensor_reduce(lmx[:, :], pr[:, :, :], AX.X, ALU.add))
                link(nc.vector.reciprocal(nt[:, :], lmx[:, :]))
                for t in range(T):
                    last = nc.vector.tensor_scalar(pr[:, t, :], pr[:, t, :], nt[:, t:t + 1], None, ALU.mult)
                last.then_inc(pr_ready.sem, 1)
                take(40)
                nc.vector.memset(work[:, N:], 2.0)
                nc.vector.tensor_copy(prT[:, :], lin[0:E, 0, 0:N])
                link(nc.vector.tensor_copy(work[:, 0:N], lin[0:E, 0, 0:N]))
                for _ in range(ROUNDS):
                    link(nc.vector.max(top8[:, :], work[:, :]))
                    link(nc.vector.match_replace(work[:, :], top8[:, :], work[:, :], -1.0))
                link(nc.vector.tensor_scalar(sel[:, :], work[:, 0:N], 0.0, None, ALU.is_lt))
                nc.vector.tensor_tensor(gate[:, :], sel[:, :], prT[:, :], ALU.mult).then_inc(free(), 1)
                nc.vector.tensor_copy(nt[:, :], nt[:, :]).then_inc(sel_ready.sem, 1)
                dve.wait_ge(lin_free["act"].sem, lin_free["act"].at(i, order(42)))
                for k in range(2):
                    last = nc.vector.tensor_scalar(yT[:, k, :], xT[:, k, :], gamma[:, k:k + 1], beta[:, k:k + 1],
                                                   ALU.mult, ALU.add)
                link(last)
                take(43)
                nc.vector.tensor_tensor(yT[:, 0, :], yT[:, 0, :], lin[0:KC, 1, 0:N], ALU.mult).then_inc(free(), 1)
                take(44)
                nc.vector.tensor_tensor(yT[:, 1, :], yT[:, 1, :], lin[0:KC, 0, 0:N], ALU.mult).then_inc(free(), 1)
                rests(1, 51)
                maxima(1, MU1, 1, N)
                sums(1)
                normalise(1, 58)
                dve.wait_ge(lin_free["act"].sem, lin_free["act"].at(i, order(62)))
                dve.wait_ge(hx_ready.sem, hx_ready.at(i, 1))
                dve.wait_ge(out_sem.sem, out_sem.at(i, 0))
                for u, t0, m in ((63, 0, 2), (64, 2, 1)):
                    take(u)
                    for t in range(m):
                        last = nc.vector.tensor_tensor(fin[:, t0 + t, :], tiles2(u % 2, P, 2)[:, t, :], b_2[:, 0, :], ALU.add)
                    last.then_inc(free(), 1)
                dve.wait_ge(free(), lin_free["dve"].at(i, order(64)))
                link(nc.vector.tensor_tensor(fin[:, :, :], fin[:, :, :], gm[:, :, :], ALU.mult))
                nc.vector.tensor_tensor(fin[:, :, :], fin[:, :, :], hx[:, :, :], ALU.add).then_inc(batch_done.sem, 1)

        @block.tensor
        def _(pe):
            mm = nc.tensor.matmul
            pe.wait_ge(loads.sem, 16 * NLOAD)
            pe.wait_ge(setup_dve.sem, 4)
            for m in range(2):
                for k in range(2):
                    last = mm(lin[0:KC, m, 0:SC], w_qkv[:, k, C + m * KC:C + (m + 1) * KC], xS[:, k, N:NK1],
                              start=k == 0, stop=k == 1)
                last.then_inc(setup_pe.sem, 1)
            for k in range(2):
                last = mm(mps[0:TK1, 0, 0:C], xS[:, k, (KT1 - 1) * TK1:NK1], w_qkv[:, k, 2 * C:], start=k == 0, stop=k == 1)
            last.then_inc(setup_pe.sem, 1)
            pe.wait_ge(setup_act.sem, 1)
            pe.wait_ge(sc_rest.sem, 2)
            pe.wait_ge(sc_pack.sem, 16 * 6)

            with pe.Fori(0, B) as i:
                def bank(u):
                    p = u - 2
                    if p >= 0:
                        s = lin_free[USES[p]]
                        pe.wait_ge(s.sem, s.at(i, order(p)))
                    else:
                        s = lin_free[USES[NU + p]]
                        pe.wait_ge(s.sem, s.at(i, 0))
                    return u % 2

                def transposes(u, src, k):
                    pe.wait_ge(ln_done.sem, ln_done.at(i, k))
                    for c in range(2):
                        b = bank(u + c)
                        for t in range(T):
                            last = nc.tensor.transpose(lin[0:KC, b, t * P:(t + 1) * P],
                                                       src[:, t, c * KC:(c + 1) * KC], ident[0:P, 0:P])
                        last.then_inc(lin_full.sem, 1)

                def freed(u):
                    s = lin_free[USES[u]]
                    pe.wait_ge(s.sem, s.at(i, order(u)))

                def by_token(u, acts, weights, rows, nt):
                    for t in range(nt):
                        if t % 2 == 0:
                            b = bank(u + t // 2)
                        out = tiles2(b, rows, 2)[:, t % 2, :]
                        for k, (x, w) in enumerate(zip(acts, weights)):
                            last = mm(out, x[:, t * rows:(t + 1) * rows], w, start=k == 0, stop=k == len(acts) - 1)
                        if t % 2 == 1 or t == nt - 1:
                            last.then_inc(lin_full.sem, 1)

                def hidden(u, x, w, bias):
                    for f in range(FT):
                        b = bank(u + f)
                        for k in range(2):
                            last = mm(lin[:, b, 0:N], w[:, k, f * 128:(f + 1) * 128], x[:, k, 0:N],
                                      start=k == 0, stop=k == 1 and not bias)
                        if bias:
                            last = mm(lin[:, b, 0:N], b_1[:, f * 128:(f + 1) * 128], sel[:, :], start=False, stop=True)
                        last.then_inc(lin_full.sem, 1)

                def queries_keys(u, x, w, c0, bias):
                    for m in range(4):
                        b = bank(u + m)
                        c = c0 + m * KC
                        for k in range(2):
                            last = mm(lin[0:KC, b, 0:N], w[:, k, c:c + KC], x[:, k, 0:N],
                                      start=k == 0, stop=k == 1 and not bias)
                        if bias:
                            last = mm(lin[0:KC, b, 0:N], b_1[:, c:c + KC], sel[:, :], start=False, stop=True)
                        last.then_inc(lin_full.sem, 1)

                def max_scores(base, halves, w):
                    n = base
                    for hd in range(H):
                        for t in range(T):
                            for s in range(halves):
                                if n >= 2:
                                    pe.wait_ge(max_free.sem, max_free.at(i, n - 1))
                                mm(mps[0:P, n % 2, 0:w], qpack[0:6 * D, hd, t * P:(t + 1) * P],
                                   kpack[0:6 * D, hd, s * w:(s + 1) * w], start=True, stop=True).then_inc(max_full.sem, 1)
                                n += 1

                def max_transposed(u, a):
                    b = bank(u)
                    pe.wait_ge(mp_ready.sem, mp_ready.at(i, a + 1))
                    pe.sem_inc(gate_pe.sem)
                    for t in range(T):
                        last = nc.tensor.transpose(lin[0:3 * H, b, t * (P // 2):(t + 1) * (P // 2)].bitcast(bf16),
                                                   mp[:, t].rearrange("p s h -> p (s h)"), identb[0:P, 0:P])
                    last.then_inc(lin_full.sem, 1)

                def attention(a, base, kt, rows, v):
                    def scores(n):
                        hd, k = 4 * (n // (4 * kt)) + n % 4, (n // 4) % kt
                        n += base
                        if n >= 3:
                            pe.wait_ge(p_ready.sem, p_ready.at(i, n - 2))
                        mm(sps[0:rows, n % 3, 0:N], kpack[0:6 * D + 3, hd, k * rows:(k + 1) * rows],
                           qpack[0:6 * D + 3, hd, :], start=True, stop=True).then_inc(s_full.sem, 1)

                    def weighted(n):
                        j, k, q = n % 4, (n // 4) % kt, n // (4 * kt)
                        hd = 4 * q + j
                        if n % (4 * kt) == 0:
                            pe.wait_ge(a_copied.sem, a_copied.at(i, GROUPS * a + q))
                        n += base
                        pe.wait_ge(p_ready.sem, p_ready.at(i, n + 1))
                        mm(aps[32 * j:32 * j + 32, 0:N], v[:, k, hd, :], prob[0:rows, n % NP, :],
                           start=k == 0, stop=k == kt - 1).then_inc(p_used.sem, 1)

                    for n in range(0, H * kt + 4, 4):
                        if n < H * kt:
                            for j in range(4):
                                scores(n + j)
                        if n >= 4:
                            for j in range(4):
                                weighted(n - 4 + j)

                def denominators(u, a):
                    for q in range(GROUPS):
                        b = bank(u + q)
                        pe.wait_ge(a_copied.sem, a_copied.at(i, GROUPS * a + q + 1))
                        mm(lin[:, b, 0:N], spread[:, :], av[:, q, :], start=True, stop=True).then_inc(lin_full.sem, 1)

                pe.wait_ge(x_in.sem, x_in.at(i, 48))
                b = bank(0)
                for t, rows in ((0, P), (1, IMG - P)):
                    for k in range(2):
                        last = mm(tiles2(b, rows, 2)[:, t, :], pT[:, k, t * P:t * P + rows], w_tok[:, k, :],
                                  start=k == 0, stop=k == 1)
                last.then_inc(lin_full.sem, 1)
                transposes(1, xn, 1)
                freed(1)
                freed(2)
                b = bank(3)
                for k in range(2):
                    last = mm(lin[0:H, b, 0:N], w_a[:, k, :], xT[:, k, :], start=k == 0, stop=k == 1)
                last.then_inc(lin_full.sem, 1)
                by_token(4, [xT[:, k, :] for k in range(2)], [w_v0[:, k, :] for k in range(2)], P, T)
                b = bank(6)
                pe.wait_ge(zs_ready.sem, zs_ready.at(i, 1))
                pe.sem_inc(gate_pe.sem)
                for t in range(T):
                    last = nc.tensor.transpose(lin[0:P, b, t * H:(t + 1) * H], zexp[:, t * P:(t + 1) * P], ident[0:H, 0:H])
                last.then_inc(lin_full.sem, 1)
                freed(4)
                freed(5)
                freed(6)
                for part in range(2):
                    b = bank(7 + part)
                    for f in range(2):
                        for t in range(T):
                            last = mm(lin[0:FW, b, 256 * f:256 * f + C + H], dft[:, t, part, f, :], vz[:, t, :],
                                      start=t == 0, stop=t == T - 1)
                    last.then_inc(lin_full.sem, 1)
                for m in range(2):
                    b = bank(9 + m)
                    if m == 0:
                        pe.wait_ge(of_ready.sem, of_ready.at(i, 1))
                    for n in range(4):
                        last = mm(lin[0:KC, b, 0:N], of[:, n // 2, n % 2, m * KC:(m + 1) * KC], idft[:, n // 2, n % 2, :],
                                  start=n == 0, stop=n == 3)
                    last.then_inc(lin_full.sem, 1)
                freed(9)
                freed(10)
                by_token(11, [aT[:, k, :] for k in range(2)], [w_p0[:, k, :] for k in range(2)], P, T)
                transposes(13, xn, 2)
                freed(13)
                freed(14)
                hidden(15, xT, w_in, False)
                freed(20)
                by_token(21, [g[:, k, :] for k in range(FT)], [w_out[:, k, :] for k in range(FT)], P, T)
                transposes(23, xn, 3)
                freed(23)
                freed(24)
                queries_keys(25, xS, w_qkv, 0, False)
                by_token(29, [xS[:, k, :] for k in range(2)], [w_qkv[:, k, 2 * C:] for k in range(2)], TK1, 4)
                pe.wait_ge(pack_in.sem, pack_in.at(i, 192))
                max_scores(0, 2, NK1 // 2)
                max_transposed(31, 0)
                pe.wait_ge(mrow_in.sem, mrow_in.at(i, 48))
                freed(30)
                attention(0, 0, KT1, TK1, v1)
                denominators(32, 0)
                pe.wait_ge(av_ready.sem, av_ready.at(i, GROUPS))
                by_token(35, [av[:, k, :] for k in range(GROUPS)], [w_p1[:, k, :] for k in range(GROUPS)], P, T)
                transposes(37, xn, 4)
                freed(37)
                freed(38)
                b = bank(39)
                for t in range(T):
                    for k in range(2):
                        last = mm(lin[0:P, b, t * E:(t + 1) * E], xT[:, k, t * P:(t + 1) * P], w_r[:, k, :],
                                  start=k == 0, stop=k == 1)
                last.then_inc(lin_full.sem, 1)
                b = bank(40)
                pe.wait_ge(pr_ready.sem, pr_ready.at(i, 1))
                for t in range(T):
                    last = nc.tensor.transpose(lin[0:E, b, t * P:(t + 1) * P], pr[:, t, :], ident[0:P, 0:P])
                last.then_inc(lin_full.sem, 1)
                transposes(41, xn5, 5)
                pe.wait_ge(sel_ready.sem, sel_ready.at(i, 1))
                for m in range(2):
                    b = bank(43 + m)
                    mm(lin[0:KC, b, 0:N], emask[:, m * KC:(m + 1) * KC], sel[:, :], start=True, stop=True).then_inc(lin_full.sem, 1)
                freed(44)
                hidden(45, yT, w_1, True)
                queries_keys(51, yT, w_1, FH, True)
                by_token(55, [yT[:, k, :] for k in range(2)] + [sel[:, :]],
                         [w_1[:, k, FH + 2 * C:] for k in range(2)] + [b_1[:, FH + 2 * C:]], P, T)
                pe.wait_ge(pack_in.sem, pack_in.at(i, 384))
                max_scores(MU1, 1, N)
                max_transposed(57, 1)
                pe.wait_ge(mrow_in.sem, mrow_in.at(i, 96))
                freed(56)
                attention(1, SU1, KT2, TK2, v2)
                denominators(58, 1)
                by_token(61, [gate[:, :]], [emask[:, :]], P, T)
                pe.wait_ge(av_ready.sem, av_ready.at(i, 2 * GROUPS))
                by_token(63, [g[:, k, :] for k in range(FT)] + [av[:, k, :] for k in range(GROUPS)],
                         [w_2[:, 0, k, :] for k in range(FT)] + [w_2a[:, 0, k, :] for k in range(GROUPS)], P, T)


def kernel(**inputs):
    import numpy as _np
    import concourse.bacc as _bacc
    from concourse import mybir as _mybir
    from concourse.bass_utils import run_bass_kernel_spmd as _run

    a = {k: _np.asarray(v) for k, v in inputs.items()}

    def rows(w, r):
        return w.reshape(-1, r, w.shape[1]).transpose(1, 0, 2)

    nh = a["x"].shape[2] // 16
    k = _np.minimum(_np.arange(2 * FW), NF)
    live = (_np.arange(2 * FW) < NF)[:, None]
    ang = 2 * _np.pi * ((k[:, None] * _np.arange(N)[None, :]) % N) / N
    both = _np.stack([_np.cos(ang) * live, _np.sin(ang) * live * ((k % (N // 2)) != 0)[:, None]])
    weight = _np.where((k % (N // 2)) == 0, 1.0, 2.0)[:, None]
    dft = both.reshape(2, 2, FW, T, P).transpose(4, 3, 0, 1, 2)
    idft = (both * weight / N).reshape(2, 2, FW, N).transpose(2, 0, 1, 3)
    width = C // 2 ** (E - 1 - _np.arange(E))
    emask = (_np.arange(C)[None, :] < width[:, None])
    spread = _np.zeros((128, 128))
    for m in range(128):
        spread[32 * (m // 32) + D, m] = 1.0
    arrays = {
        "x": a["x"].reshape(B, nh, 16, nh, 16).transpose(0, 2, 4, 1, 3).reshape(B, 2, 128, IMG).transpose(0, 2, 1, 3),
        "txt": a["txt"],
        "w_tok": rows(a["L0_tok_W"].T, 128),
        "w_a": rows(a["L0_attn_W_A"], KC),
        "w_v0": rows(a["L0_attn_W_V"], KC),
        "w_p0": rows(a["L0_attn_W_proj"], KC),
        "b_p0": a["L0_attn_b_proj"],
        "w_in": rows(a["L0_ffn_in_weight"].T, KC),
        "b_in": a["L0_ffn_in_bias"].reshape(FT, 128).T,
        "w_out": rows(a["L0_ffn_out_weight"], 128),
        "sc": rows(a["L1_attn_sc_token"][0].T, KC),
        "w_qkv": rows(a["L1_attn_W_qkv"], KC),
        "w_p1": a["L1_attn_W_proj"],
        "b_p1": a["L1_attn_b_proj"],
        "w_r": rows(a["L1_ffn_w_router"].T, KC),
        "gamma": a["L1_ffn_gamma1"].reshape(2, KC).T,
        "beta": a["L1_ffn_beta1"].reshape(2, KC).T,
        "w_1": rows(a["L1_ffn_w1"].T, KC),
        "b_1": a["L1_ffn_b1"].reshape(1, -1),
        "w_2": a["L1_ffn_w2"][:, :FH].reshape(2, C, FT, 128).transpose(3, 0, 2, 1),
        "w_2a": a["L1_ffn_w2"][:, FH:].reshape(2, C, C).transpose(0, 2, 1),
        "b_2": a["L1_ffn_b2"].reshape(2, C),
        "ident": _np.eye(128, dtype=_np.float32),
        "dft": dft.astype(_np.float32),
        "idft": idft.astype(_np.float32),
        "spread": spread.astype(_np.float32),
        "emask": emask.astype(_np.float32),
    }
    nc = _bacc.Bacc("TRN2", target_bir_lowering=False, num_devices=1)
    ins, aps = {}, {}
    for name, v in arrays.items():
        v = _np.ascontiguousarray(v)
        ins[f"in_{name}"] = v
        aps[name] = nc.dram_tensor(f"in_{name}", v.shape, _mybir.dt.from_np(v.dtype), kind="ExternalInput").ap()
    aps["out"] = nc.dram_tensor("out_0", (B, N, C), _mybir.dt.float32, kind="ExternalOutput").ap()
    build(nc, aps)
    r = _run(nc, [ins], core_ids=[0])
    return r.results[0]["out_0"]
```

```python
import numpy as np
import concourse.bass as bass
from concourse import mybir
from contextlib import ExitStack

B = 16
IMG, TXT, SC = 196, 128, 196
N = IMG + TXT
C = 192
P, T = 108, 3
KC = 96
H, D = 12, 16
NK1 = N + SC
TK1, KT1 = 104, 5
TK2, KT2 = P, T
FH = 768
FT = FH // 128
E, CAP = 4, N // 2
PAD = 8 * ((CAP + 7) // 8) - CAP
ROUNDS = (CAP + PAD) // 8
NF = N // 2 + 1
FW = 82
SCALE = float(D) ** -0.5
Q_PARTS = (0, 0, 0, 1, 1, 2)
K_PARTS = (0, 1, 2, 0, 1, 0)
GROUPS = 3


class Ring:

    def __init__(self, name, banks, uses, signal):
        self.banks, self.uses = banks, uses
        self.full = signal(name + "_full", len(uses))
        self.free = {e: signal(f"{name}_free_{e}", uses.count(e)) for e in sorted(set(uses))}

    def order(self, u):
        return self.uses[:u + 1].count(self.uses[u])

    def filled(self, eng, j, u):
        eng.wait_ge(self.full.sem, self.full.at(j, u + 1))

    def emptied(self, eng, j, u):
        s = self.free[self.uses[u]]
        eng.wait_ge(s.sem, s.at(j, self.order(u)))

    def bank(self, eng, j, u):
        if u >= 2:
            self.emptied(eng, j, u - 2)
        else:
            p = len(self.uses) - 1
            while p % 2 != u % 2:
                p -= 1
            s = self.free[self.uses[p]]
            eng.wait_ge(s.sem, s.at(j, 0))
        return self.banks[:, u % 2, :]

    def at(self, u):
        return self.banks[:, u % 2, :]


class Signal:

    def __init__(self, sem, per, primed=1):
        self.sem, self.per, self.primed = sem, per, primed

    def at(self, i, n):
        return (i + self.primed) * self.per + n


def build(nc, A):
    fp32, bf16, i32 = mybir.dt.float32, mybir.dt.bfloat16, mybir.dt.int32
    ALU, ACT, AX = mybir.AluOpType, mybir.ActivationFunctionType, mybir.AxisListType
    ctx = ExitStack()
    with ctx:
        def sb(name, shape, dt=fp32):
            return ctx.enter_context(nc.sbuf_tensor(name, shape, dt))

        primed = []

        def signal(name, per=1, prime=1):
            s = Signal(ctx.enter_context(nc.semaphore(name)), per, prime)
            if per and prime:
                primed.append(s)
            return s

        w_tok = sb("w_tok", [128, 2, C])
        w_a = sb("w_a", [KC, 2, H])
        w_v0 = sb("w_v0", [KC, 2, C])
        w_p0 = sb("w_p0", [KC, 2, C])
        b_p0 = sb("b_p0", [P, C])
        w_in = sb("w_in", [KC, 2, FH])
        b_in = sb("b_in", [128, FT])
        w_out = sb("w_out", [128, FT, C])
        w_qkv = sb("w_qkv", [KC, 2, 3 * C])
        w_p1 = sb("w_p1", [128, GROUPS, C])
        b_p1 = sb("b_p1", [P, C])
        w_r = sb("w_r", [KC, 2, E])
        gamma = sb("gamma", [KC, 2])
        beta = sb("beta", [KC, 2])
        w_1 = sb("w_1", [KC, 2, FH + 3 * C])
        b_1 = sb("b_1", [E, FH + 3 * C])
        w_2 = sb("w_2", [128, 2, FT, C])
        w_2a = sb("w_2a", [128, 2, GROUPS, C])
        b_2 = sb("b_2", [P, 2, C])
        ident = sb("ident", [128, 128])
        identb = sb("identb", [128, 128], bf16)
        dft = sb("dft", [P, T, 2, 2, FW])
        idft = sb("idft", [FW, 2, 2, N])
        spread = sb("spread", [128, 128])
        emask = sb("emask", [E, C])

        pT = sb("pT", [128, 2, IMG])
        hin = sb("hin", [P, T, C])
        hb = sb("hb", [P, T, C])
        h = sb("h", [P, T, C])
        xn = sb("xn", [P, T, C])
        st = sb("st", [P, T, 6])
        mv = sb("mv", [P, T, 2])
        var = sb("var", [P, T])
        rs = sb("rs", [P, T])
        nt = sb("nt", [P, T])
        xT = sb("xT", [KC, 2, N])
        xS = sb("xS", [KC, 2, NK1])
        nmz = sb("nmz", [H, 1])
        zsum = sb("zsum", [H, 1])
        zrec = sb("zrec", [H, 1])
        zexp = sb("zexp", [H, N])
        vz = sb("vz", [P, T, C + H])
        zf = sb("zf", [FW, 2, 2, H])
        ta = sb("ta", [FW, 2, C])
        tb = sb("tb", [FW, 2, C])
        of = sb("of", [FW, 2, 2, C])
        aT = sb("aT", [KC, 2, N])
        g = sb("g", [128, FT, N])
        piece = sb("piece", [KC, 4, 3, N], bf16)
        rest = sb("rest", [KC, 4, N])
        qpack = sb("qpack", [6 * D + 3, H, N], bf16)
        kpack = sb("kpack", [6 * D + 3, H, NK1], bf16)
        v1 = sb("v1", [TK1, KT1, H, 32])
        v2 = sb("v2", [TK2, KT2, H, 32])
        mxh = sb("mxh", [P, 4, T, 2])
        mx = sb("mx", [P, T, 4])
        mr = sb("mr", [P, T, 4])
        mp = sb("mp", [P, T, 3, 4], bf16)
        mT = sb("mT", [12, N], bf16)
        NP = 12
        prob = sb("prob", [128, NP, N])
        av = sb("av", [128, GROUPS, N])
        rc = sb("rc", [128, N])
        ha = sb("ha", [P, T, C])
        hab = sb("hab", [P, T, C])
        xna = sb("xna", [P, T, C])
        xn5 = sb("xn5", [P, T, C])
        xTa = sb("xTa", [KC, 2, N])
        lg = sb("lg", [P, T, E])
        lmx = sb("lmx", [P, T])
        nta = sb("nta", [P, T])
        pr = sb("pr", [P, T, E])
        prT = sb("prT", [E, N])
        hx = sb("hx", [P, T, C])
        yA = sb("yA", [KC, 2, N])
        pall = sb("pall", [B * E, N])
        work = sb("work", [B * E, N + PAD])
        top8 = sb("top8", [B * E, 8])
        selall = sb("selall", [B * E, N])
        gateall = sb("gateall", [B * E, N])
        sel = sb("sel", [E, N])
        gate = sb("gate", [E, N])
        yT = sb("yT", [KC, 2, N])
        gm = sb("gm", [P, T, C])
        acc = sb("acc", [P, T, C])
        hxb = sb("hxb", [P, T, C])
        fin = sb("fin", [P, T, C])

        lin = ctx.enter_context(nc.psum_tensor("lin", [128, 2, 512], fp32))
        mps = ctx.enter_context(nc.psum_tensor("mps", [128, 2, 512], fp32))
        sps = ctx.enter_context(nc.psum_tensor("sps", [128, 3, 512], fp32))
        aps = ctx.enter_context(nc.psum_tensor("aps", [128, 512], fp32))

        def dram(name, shape, dt=fp32):
            return nc.dram_tensor(name, shape, dt, kind="Internal").ap()

        scr = dram("scr", (2, 3, C, N), bf16)
        hx_d = dram("hx_d", (B, P, T, C))
        y_d = dram("y_d", (B, KC, 2, N))
        pr_d = dram("pr_d", (B * E, N))
        sel_d = dram("sel_d", (B, E, N))
        gate_d = dram("gate_d", (B, E, N))

        F_TOK, F_T1, F_Z, F_V, F_ZT, F_DFT, F_INV, F_PROJ, F_T2, F_HID, F_OUT, F_T3, F_QK, F_VAL = (
            0, 1, 3, 4, 6, 7, 9, 11, 13, 15, 21, 23, 25, 29)
        front = Ring("front", lin, ["act"] * 3 + ["dve"] + ["act"] * 2 + ["dve"] * 3 + ["act"] * 2 + ["dve"] * 2
                     + ["act"] * 8 + ["dve"] * 2 + ["act"] * 2 + ["dve"] * 4 + ["act"] * 2, signal)
        MU1, MU2 = 4 * T * 2, 4 * T
        R_DEN = GROUPS * (MU1 + 1)
        R_PROJ, R_T4, R_LOG, R_PRT, R_T5 = R_DEN + 3, R_DEN + 5, R_DEN + 7, R_DEN + 8, R_DEN + 9
        back = Ring("back", mps, (["dve"] * MU1 + ["act"]) * GROUPS + ["dve"] * 5 + ["act"] * 2 + ["dve"] * 2
                    + ["act"] * 2, signal)
        M_CNT, M_HID, M_QK, M_VAL = 0, 2, 8, 12
        moe = Ring("moe", lin, ["dve"] * 2 + ["act"] * 6 + ["dve"] * 4 + ["act"] * 2, signal)
        moe_out = Ring("moe_out", lin, ["dve"] * 2, signal)
        O_DEN = GROUPS * (MU2 + 1)
        O_GATE, O_PROJ = O_DEN + 3, O_DEN + 5
        last = Ring("last", mps, (["dve"] * MU2 + ["act"]) * GROUPS + ["dve"] * 3 + ["act"] * 2 + ["dve"] * 2, signal)

        class Attention:

            def __init__(self, name, ring, kt, rows, mu, halves, den, values):
                self.ring, self.kt, self.rows, self.mu, self.halves, self.den = ring, kt, rows, mu, halves, den
                self.values = values
                self.width = N if halves == 1 else NK1 // 2
                self.units = H * kt
                self.scored = signal(name + "_scored", self.units)
                self.exped = signal(name + "_exped", self.units)
                self.summed = signal(name + "_summed", self.units)
                self.copied = signal(name + "_copied", GROUPS)
                self.maxed = signal(name + "_maxed", GROUPS)
                self.rows_in = signal(name + "_rows_in", 48 * GROUPS)
                self.normed = signal(name + "_normed", GROUPS)
                self.first = signal(name + "_first", 4)
                self.third = signal(name + "_third", 4)
                self.second = signal(name + "_second", 4)
                self.scr_in = signal(name + "_scr_in", 64)
                self.pack_in = signal(name + "_pack_in", 192)

        one = Attention("own_shared", back, KT1, TK1, MU1, 2, R_DEN, v1)
        two = Attention("own", last, KT2, TK2, MU2, 1, O_DEN, v2)

        loads, setup_dve, setup_pe, setup_act, setup_pool, sc_first, sc_rest, sc_mid, sc_pieces, sc_scr, sc_pack = (
            signal(n, 0) for n in ("loads", "setup_dve", "setup_pe", "setup_act", "setup_pool", "sc_first",
                                   "sc_rest", "sc_mid", "sc_pieces", "sc_scr", "sc_pack"))
        x_in = signal("x_in", 48, prime=0)
        hb_ready = signal("hb_ready")
        hab_ready = signal("hab_ready")
        ln_done = signal("ln_done", 3)
        lna_done = signal("lna_done", 2)
        nmz_ready = signal("nmz_ready")
        zexp_ready = signal("zexp_ready")
        zs_ready = signal("zs_ready")
        of_ready = signal("of_ready")
        lg_ready = signal("lg_ready")
        pe_ready = signal("pe_ready")
        pr_ready = signal("pr_ready")
        hx_ready = signal("hx_ready")
        spilled = signal("spilled", 48)
        picks_in = signal("picks_in", 0)
        picked = signal("picked", 0)
        picks_out = signal("picks_out", 0)
        moe_in = signal("moe_in", 32)
        tail_in = signal("tail_in", 32)
        yT_ready = signal("yT_ready", 2)
        fin_ready = signal("fin_ready")
        stored = signal("stored", 16)
        dve_link = signal("dve_link", 0)
        gate_pe, gate_pool, gate_sp = signal("gate_pe", 0), signal("gate_pool", 0), signal("gate_sp", 0)

        block = ctx.enter_context(nc.Block())

        LOADS = [
            (w_tok, A["w_tok"]), (w_a, A["w_a"]), (w_v0, A["w_v0"]), (w_p0, A["w_p0"]),
            (w_in, A["w_in"]), (b_in, A["b_in"]), (w_out, A["w_out"]), (w_qkv, A["w_qkv"]),
            (w_r, A["w_r"]), (gamma, A["gamma"]), (beta, A["beta"]), (w_1, A["w_1"]),
            (w_2, A["w_2"]), (ident, A["ident"]), (dft, A["dft"]), (idft, A["idft"]),
            (spread, A["spread"]), (emask, A["emask"])]
        NLOAD = len(LOADS) + 3 * H + E + 3 + 1

        def tiles2(bank):
            return bank.rearrange("p (t c) -> p t c", t=2)[:, :, 0:C]

        def attention_slots(att):
            return ["max0", "max1"] + list(range(GROUPS * att.kt)) + ["end"]

        def max_units(att, slot):
            half = att.mu // 2
            if slot == "max0":
                return 0, range(0, half), False
            if slot == "max1":
                return 0, range(half, att.mu), True
            if slot == "end":
                return None
            q, k = divmod(slot, att.kt)
            parts = att.kt - 1
            if q == GROUPS - 1 or k == parts:
                return None
            size = att.mu // parts
            return q + 1, range(k * size, (k + 1) * size), k == parts - 1

        FRONT = {"max1": ["tok"], 0: ["t1"], 1: ["zv"], 2: ["zt"], 3: ["dft"], 5: ["inv"], 6: ["proj"],
                 8: ["t2"], 9: ["hidden"], 10: ["out"], 12: ["t3"], 13: ["qk"], "end": ["values"]}
        FRONT_ALL = [x for v in FRONT.values() for x in v]
        MOE = {"max0": ["out0"], "max1": ["out1"], 0: ["count"], 2: ["hidden"], 6: ["qk"], "end": ["values"]}
        MOE_ALL = ["count", "hidden", "qk", "values"]

        @block.sync
        def _(sp):
            for s in primed:
                sp.sem_inc(s.sem, s.per)
            for dst, src in LOADS:
                sp.dma_start(dst.ap(), src).then_inc(loads.sem, 16)
            sp.wait_ge(setup_pool.sem, 2)
            for hd in range(H):
                r = 32 * (hd % 4)
                sp.dma_start(w_p1[r:r + D, hd // 4, :], A["w_p1"][hd * D:(hd + 1) * D, :]).then_inc(loads.sem, 16)
                for s in range(2):
                    sp.dma_start(w_2a[r:r + D, s, hd // 4, :],
                                 A["w_2a"][s, hd * D:(hd + 1) * D, :]).then_inc(loads.sem, 16)
            for e in range(E):
                sp.dma_start(b_1[e:e + 1, :], A["b_1"]).then_inc(loads.sem, 16)
            sp.dma_start(b_p0[:, :], A["b_p0"].partition_broadcast(P)).then_inc(loads.sem, 16)
            sp.dma_start(b_p1[:, :], A["b_p1"].partition_broadcast(P)).then_inc(loads.sem, 16)
            sp.dma_start(b_2[:, :, :], A["b_2"].partition_broadcast(P)).then_inc(loads.sem, 16)
            sp.dma_start(xS[:, :, N:NK1], A["sc"]).then_inc(loads.sem, 16)
            sp.wait_ge(sc_pieces.sem, 2)
            for m in range(2):
                sp.dma_start(scr[1, :, m * KC:(m + 1) * KC, 0:SC].rearrange("s p n -> p s n"),
                             piece[:, 2 + m, :, 0:SC]).then_inc(sc_scr.sem, 16)
            sp.wait_ge(sc_scr.sem, 32)
            for r, s in enumerate(K_PARTS):
                sp.dma_start(kpack[r * D:(r + 1) * D, :, N:NK1],
                             scr[1, s, :, 0:SC].rearrange("(h d) n -> d h n", d=D)).then_inc(sc_pack.sem, 16)
            sp.wait_ge(sc_pack.sem, 16 * 6)

            def pack(att, j):
                for m in range(4):
                    sp.wait_ge(att.third.sem, att.third.at(j, m + 1))
                    sp.dma_start(scr[m // 2, :, (m % 2) * KC:(m % 2 + 1) * KC, :].rearrange("s p n -> p s n"),
                                 piece[:, m, :, :]).then_inc(att.scr_in.sem, 16)
                sp.wait_ge(att.scr_in.sem, att.scr_in.at(j, 64))
                sp.sem_inc(gate_sp.sem)
                sp.wait_ge(att.exped.sem, att.exped.at(j, 0))
                for r in range(6):
                    sp.dma_start(qpack[r * D:(r + 1) * D, :, :],
                                 scr[0, Q_PARTS[r], :, :].rearrange("(h d) n -> d h n", d=D)).then_inc(att.pack_in.sem, 16)
                    sp.dma_start(kpack[r * D:(r + 1) * D, :, 0:N],
                                 scr[1, K_PARTS[r], :, :].rearrange("(h d) n -> d h n", d=D)).then_inc(att.pack_in.sem, 16)

            def max_rows(att, i):
                for q in range(GROUPS):
                    att.ring.emptied(sp, i, (q + 1) * (att.mu + 1) - 1)
                    for s in range(3):
                        sp.dma_start(qpack[6 * D + s:6 * D + s + 1, 4 * q:4 * q + 4, :],
                                     mT[4 * s:4 * s + 4, :]).then_inc(att.rows_in.sem, 16)

            def first_loop(i, with_front):
                max_rows(one, i)
                if with_front:
                    pack(one, i + 1)
                sp.wait_ge(hx_ready.sem, hx_ready.at(i, 1))
                sp.dma_start(hx_d[i], hx[:, :, :]).then_inc(spilled.sem, 16)
                back.emptied(sp, i, R_PRT)
                sp.dma_start(pr_d[bass.ds(i * E, E), :], prT[:, :]).then_inc(spilled.sem, 16)
                back.emptied(sp, i, R_T5 + 1)
                sp.dma_start(y_d[i], yA[:, :, :]).then_inc(spilled.sem, 16)

            pack(one, 0)
            with sp.Fori(0, B - 1) as i:
                first_loop(i, True)
            first_loop(B - 1, False)
            sp.wait_ge(spilled.sem, spilled.at(B - 1, 48))
            sp.dma_start(pall[:, :], pr_d[:, :]).then_inc(picks_in.sem, 16)
            sp.wait_ge(picked.sem, 2)
            sp.dma_start(sel_d.rearrange("b e n -> (b e) n"), selall[:, :]).then_inc(picks_out.sem, 16)
            sp.dma_start(gate_d.rearrange("b e n -> (b e) n"), gateall[:, :]).then_inc(picks_out.sem, 16)
            sp.wait_ge(picks_out.sem, 32)

            def load_moe(j):
                moe.filled(sp, j - 1, M_VAL + 1)
                sp.dma_start(yT[:, :, :], y_d[j]).then_inc(moe_in.sem, 16)
                sp.dma_start(sel[:, :], sel_d[j]).then_inc(moe_in.sem, 16)

            def second_loop(i, with_moe):
                if with_moe:
                    load_moe(i + 1)
                sp.wait_ge(fin_ready.sem, fin_ready.at(i, 0))
                sp.dma_start(gate[:, :], gate_d[i]).then_inc(tail_in.sem, 16)
                sp.dma_start(hxb[:, :, :], hx_d[i]).then_inc(tail_in.sem, 16)
                max_rows(two, i)
                if with_moe:
                    pack(two, i + 1)
                sp.wait_ge(fin_ready.sem, fin_ready.at(i, 1))
                sp.dma_start(A["out"][i].rearrange("(t p) c -> p t c", p=P), fin[:, :, :]).then_inc(stored.sem, 16)

            load_moe(0)
            pack(two, 0)
            with sp.Fori(0, B - 1) as i:
                second_loop(i, True)
            second_loop(B - 1, False)
            sp.wait_ge(stored.sem, stored.at(B - 1, 16))

        @block.gpsimd
        def _(pool):
            nc.gpsimd.memset(w_p1[:, :, :], 0.0).then_inc(setup_pool.sem, 1)
            nc.gpsimd.memset(w_2a[:, :, :, :], 0.0).then_inc(setup_pool.sem, 1)
            nc.gpsimd.memset(v1[:, :, :, :], 0.0).then_inc(setup_pool.sem, 1)
            nc.gpsimd.memset(v2[:, :, :, :], 0.0).then_inc(setup_pool.sem, 1)
            pool.wait_ge(setup_pool.sem, 4)
            nc.gpsimd.memset(v1[:, :, :, D:D + 1], 1.0).then_inc(setup_pool.sem, 1)
            nc.gpsimd.memset(v2[:, :, :, D:D + 1], 1.0).then_inc(setup_pool.sem, 1)
            pool.wait_ge(setup_pool.sem, 6)
            nc.gpsimd.memset(kpack[6 * D:6 * D + 3, :, :], 1.0).then_inc(setup_pool.sem, 1)
            for m in range(2, 4):
                pool.wait_ge(sc_rest.sem, m - 1)
                nc.gpsimd.tensor_copy(piece[:, m, 1, 0:SC], rest[:, m, 0:SC]).then_inc(sc_mid.sem, 1)
                pool.wait_ge(sc_mid.sem, m - 1)
                nc.gpsimd.tensor_tensor(piece[:, m, 2, 0:SC], rest[:, m, 0:SC], piece[:, m, 1, 0:SC],
                                        ALU.subtract).then_inc(sc_pieces.sem, 1)
            pool.wait_ge(loads.sem, 16 * NLOAD)

            def load_x(j):
                front.filled(pool, j - 1, F_TOK)
                front.emptied(pool, j - 1, F_PROJ)
                pool.dma_start(pT[:, :, :], A["x"][j]).then_inc(x_in.sem, 16)
                pool.dma_start(hin[IMG - P:P, 1, :], A["txt"][j, 0:2 * P - IMG, :]).then_inc(x_in.sem, 16)
                pool.dma_start(hin[:, 2, :], A["txt"][j, 2 * P - IMG:TXT, :]).then_inc(x_in.sem, 16)

            def biased_input(j):
                front.emptied(pool, j, F_TOK)
                pool.wait_ge(x_in.sem, x_in.at(j, 48))
                for t in range(T):
                    done = nc.gpsimd.tensor_tensor(hb[:, t, :], hin[:, t, :], b_p0[:, :], ALU.add)
                done.then_inc(hb_ready.sem, 1)

            def biased_residual(j):
                front.emptied(pool, j, F_OUT + 1)
                back.emptied(pool, j - 1, R_PROJ + 1)
                for t in range(T):
                    done = nc.gpsimd.tensor_tensor(hab[:, t, :], h[:, t, :], b_p1[:, :], ALU.add)
                done.then_inc(hab_ready.sem, 1)

            def parts(att, ring, u, j):
                for m in range(4):
                    ring.emptied(pool, j, u + m)
                    pool.wait_ge(att.scr_in.sem, att.scr_in.at(j, 0))
                    pool.sem_inc(gate_pool.sem)
                    nc.gpsimd.tensor_copy(piece[:, m, 1, :], rest[:, m, :]).then_inc(att.second.sem, 1)
                    pool.wait_ge(att.second.sem, att.second.at(j, m + 1))
                    nc.gpsimd.tensor_tensor(piece[:, m, 2, :], rest[:, m, :], piece[:, m, 1, :],
                                            ALU.subtract).then_inc(att.third.sem, 1)

            load_x(0)
            biased_input(0)
            parts(one, front, F_QK, 0)
            biased_residual(0)

            def first_loop(i, with_front):
                if with_front:
                    load_x(i + 1)
                    biased_input(i + 1)
                    parts(one, front, F_QK, i + 1)
                pool.wait_ge(lna_done.sem, lna_done.at(i, 1))
                pool.wait_ge(spilled.sem, spilled.at(i, 0))
                nc.gpsimd.tensor_tensor(hx[:, :, :], ha[:, :, :], xna[:, :, :], ALU.add).then_inc(hx_ready.sem, 1)
                if with_front:
                    biased_residual(i + 1)

            with pool.Fori(0, B - 1) as i:
                first_loop(i, True)
            first_loop(B - 1, False)
            parts(two, moe, M_QK, 0)
            with pool.Fori(0, B - 1) as i:
                parts(two, moe, M_QK, i + 1)
            pool.wait_ge(x_in.sem, x_in.at(B - 1, 48))

        @block.scalar
        def _(act):
            act.wait_ge(loads.sem, 16 * NLOAD)
            for m in range(2):
                act.wait_ge(setup_pe.sem, m + 1)
                nc.scalar.copy(piece[:, 2 + m, 0, 0:SC], lin[0:KC, m, 0:SC]).then_inc(sc_first.sem, 1)
            act.wait_ge(setup_pe.sem, 3)
            act.wait_ge(setup_pool.sem, 7)
            nc.scalar.copy(v1[:, KT1 - 1, :, 0:D],
                           mps[0:TK1, 0, 0:C].rearrange("p (h d) -> p h d", d=D)).then_inc(setup_act.sem, 1)

            def transposed(ring, j, u, dst):
                for k in range(2):
                    ring.filled(act, j, u + k)
                    nc.scalar.copy(dst[:, k, 0:N], ring.at(u + k)[0:KC, 0:N]).then_inc(ring.free["act"].sem, 1)

            def hidden(ring, j, u, bias):
                for f in range(FT):
                    ring.filled(act, j, u + f)
                    nc.scalar.activation(g[:, f, :], ring.at(u + f)[:, 0:N], ACT.Gelu,
                                         bias=b_in[:, f:f + 1] if bias else 0.0).then_inc(ring.free["act"].sem, 1)

            def first_parts(att, ring, j, u):
                for m in range(4):
                    ring.filled(act, j, u + m)
                    act.wait_ge(att.scr_in.sem, att.scr_in.at(j, 0))
                    nc.scalar.copy(piece[:, m, 0, :], ring.at(u + m)[0:KC, 0:N]).then_inc(att.first.sem, 1)

            def values(att, ring, j, u, nt):
                act.wait_ge(att.summed.sem, att.summed.at(j, 0))
                for k in range((nt + 1) // 2):
                    ring.filled(act, j, u + k)
                    for s in range(min(2, nt - 2 * k)):
                        done = nc.scalar.copy(att.values[:, 2 * k + s, :, 0:D],
                                              tiles2(ring.at(u + k))[0:att.rows, s, :].rearrange("p (h d) -> p h d", d=D))
                    done.then_inc(ring.free["act"].sem, 1)

            def front_step(j, step):
                if step == "tok":
                    front.filled(act, j, F_TOK)
                    act.wait_ge(x_in.sem, x_in.at(j, 48))
                    nc.scalar.copy(hin[:, 0, :], lin[0:P, 0, 0:C])
                    nc.scalar.copy(hin[0:IMG - P, 1, :], lin[0:IMG - P, 0, 256:256 + C]).then_inc(front.free["act"].sem, 1)
                elif step == "t1":
                    transposed(front, j, F_T1, xT)
                elif step == "zv":
                    act.wait_ge(nmz_ready.sem, nmz_ready.at(j, 1))
                    nc.scalar.activation(zexp[:, :], front.at(F_Z)[0:H, 0:N], ACT.Exp, bias=nmz[:, 0:1],
                                         accum_out=zsum[:, 0:1]).then_inc(zexp_ready.sem, 1)
                    front.filled(act, j, F_V)
                    nc.scalar.copy(vz[:, 0:2, 0:C], tiles2(front.at(F_V))[0:P]).then_inc(front.free["act"].sem, 1)
                    front.filled(act, j, F_V + 1)
                    nc.scalar.copy(vz[:, 2:3, 0:C], tiles2(front.at(F_V + 1))[0:P, 0:1]).then_inc(front.free["act"].sem, 1)
                elif step == "inv":
                    transposed(front, j, F_INV, aT)
                elif step == "t2":
                    transposed(front, j, F_T2, xT)
                elif step == "hidden":
                    hidden(front, j, F_HID, True)
                elif step == "t3":
                    transposed(front, j, F_T3, xS)
                elif step == "qk":
                    first_parts(one, front, j, F_QK)
                elif step == "values":
                    values(one, front, j, F_VAL, 4)

            def attention_step(att, i, slot):
                if isinstance(slot, int):
                    for n in range(4 * slot, 4 * slot + 4):
                        act.wait_ge(att.scored.sem, att.scored.at(i, n + 1))
                        act.wait_ge(att.summed.sem, att.summed.at(i, n - NP + 1))
                        nc.scalar.activation(prob[0:att.rows, n % NP, :], sps[0:att.rows, n % 3, 0:N], ACT.Exp,
                                             scale=SCALE).then_inc(att.exped.sem, 1)
                w = max_units(att, slot)
                if w and w[2]:
                    u = (w[0] + 1) * (att.mu + 1) - 1
                    att.ring.filled(act, i, u)
                    act.wait_ge(att.rows_in.sem, att.rows_in.at(i, 48 * w[0]))
                    nc.scalar.copy(mT[:, :], att.ring.at(u)[0:12, 0:N // 2].bitcast(bf16)).then_inc(att.ring.free["act"].sem, 1)

            def first_loop(i, with_front):
                for slot in attention_slots(one):
                    attention_step(one, i, slot)
                    if with_front:
                        for step in FRONT.get(slot, ()):
                            front_step(i + 1, step)
                transposed(back, i, R_T4, xTa)
                act.wait_ge(lg_ready.sem, lg_ready.at(i, 1))
                nc.scalar.activation(pr[:, :, :], lg[:, :, :], ACT.Exp).then_inc(pe_ready.sem, 1)
                act.wait_ge(spilled.sem, spilled.at(i, 0))
                for k in range(2):
                    back.filled(act, i, R_T5 + k)
                    nc.scalar.activation(yA[:, k, :], back.at(R_T5 + k)[0:KC, 0:N], ACT.Identity,
                                         bias=beta[:, k:k + 1], scale=gamma[:, k:k + 1]).then_inc(back.free["act"].sem, 1)

            for step in FRONT_ALL:
                front_step(0, step)
            with act.Fori(0, B - 1) as i:
                first_loop(i, True)
            first_loop(B - 1, False)

            def moe_step(j, step):
                if step == "hidden":
                    moe_out.filled(act, j - 1, 1)
                    hidden(moe, j, M_HID, False)
                elif step == "qk":
                    first_parts(two, moe, j, M_QK)
                elif step == "values":
                    values(two, moe, j, M_VAL, 3)

            def second_loop(i, with_moe):
                for slot in attention_slots(two):
                    attention_step(two, i, slot)
                    if with_moe:
                        for step in MOE.get(slot, ()):
                            moe_step(i + 1, step)
                act.wait_ge(fin_ready.sem, fin_ready.at(i, 0))
                last.filled(act, i, O_GATE)
                nc.scalar.copy(gm[:, 0:2, :], tiles2(last.at(O_GATE))[0:P]).then_inc(last.free["act"].sem, 1)
                last.filled(act, i, O_GATE + 1)
                nc.scalar.copy(gm[:, 2:3, :], tiles2(last.at(O_GATE + 1))[0:P, 0:1]).then_inc(last.free["act"].sem, 1)

            for step in MOE_ALL:
                moe_step(0, step)
            with act.Fori(0, B - 1) as i:
                second_loop(i, True)
            second_loop(B - 1, False)

        @block.vector
        def _(dve):
            dve.wait_ge(loads.sem, 16 * NLOAD)
            nc.vector.tensor_copy(identb[:, :], ident[:, :]).then_inc(setup_dve.sem, 1)
            nc.vector.tensor_tensor(w_2[:, 0], w_2[:, 0], w_2[:, 1], ALU.add).then_inc(setup_dve.sem, 1)
            nc.vector.tensor_tensor(w_2a[:, 0], w_2a[:, 0], w_2a[:, 1], ALU.add).then_inc(setup_dve.sem, 1)
            nc.vector.tensor_tensor(b_2[:, 0], b_2[:, 0], b_2[:, 1], ALU.add).then_inc(setup_dve.sem, 1)
            for m in range(2):
                dve.wait_ge(sc_first.sem, m + 1)
                nc.vector.tensor_tensor(rest[:, 2 + m, 0:SC], lin[0:KC, m, 0:SC], piece[:, 2 + m, 0, 0:SC],
                                        ALU.subtract).then_inc(sc_rest.sem, 1)
            dve.wait_ge(setup_dve.sem, 4)
            dve.wait_ge(sc_pieces.sem, 2)
            links = [0]

            def link(ins):
                links[0] += 1
                ins.then_inc(dve_link.sem, 1)
                dve.wait_ge(dve_link.sem, links[0])

            def restart():
                links[0] = 0
                dve.sem_clear(dve_link.sem)

            def layernorm(src, dst, eps, signals):
                for t in range(T):
                    done = nc.vector.bn_stats(st[:, t, :], src[:, t, :])
                link(done)
                for t in range(T):
                    done = nc.vector.bn_aggr(mv[:, t, :], st[:, t, :])
                link(done)
                link(nc.vector.tensor_scalar(var[:, :], mv[:, :, 1], eps, None, ALU.add))
                link(nc.vector.tensor_scalar(rs[:, :].bitcast(i32), var[:, :].bitcast(i32), -0.5, 1597463007.0,
                                             ALU.mult, ALU.add))
                for _ in range(4):
                    link(nc.vector.tensor_tensor(nt[:, :], rs[:, :], rs[:, :], ALU.mult))
                    link(nc.vector.scalar_tensor_tensor(nt[:, :], nt[:, :], -0.5, var[:, :], ALU.mult, ALU.mult))
                    link(nc.vector.scalar_tensor_tensor(rs[:, :], nt[:, :], 1.5, rs[:, :], ALU.add, ALU.mult))
                for t in range(T):
                    done = nc.vector.tensor_scalar(dst[:, t, :], src[:, t, :], mv[:, t, 0:1], rs[:, t:t + 1],
                                                   ALU.subtract, ALU.mult)
                done.then_inc(signals.sem, 1)

            def residual(ring, j, u, dst, add):
                for k in range(2):
                    ring.filled(dve, j, u + k)
                    t = slice(0, 2) if k == 0 else slice(2, 3)
                    nc.vector.tensor_tensor(dst[:, t, :], tiles2(ring.at(u + k))[0:P, 0:2 - k, :], add[:, t, :],
                                            ALU.add).then_inc(ring.free["dve"].sem, 1)
                ring.emptied(dve, j, u + 1)

            def rests(att, ring, j, u):
                for m in range(4):
                    ring.filled(dve, j, u + m)
                    dve.wait_ge(att.first.sem, att.first.at(j, m + 1))
                    dve.wait_ge(att.third.sem, att.third.at(j, 0))
                    nc.vector.tensor_tensor(rest[:, m, :], ring.at(u + m)[0:KC, 0:N], piece[:, m, 0, :],
                                            ALU.subtract).then_inc(ring.free["dve"].sem, 1)

            def front_step(j, step):
                free = front.free["dve"].sem
                if step == "tok":
                    front.emptied(dve, j, F_TOK)
                    layernorm(hin, xn, 1e-5, ln_done)
                elif step == "zv":
                    front.filled(dve, j, F_Z)
                    nc.vector.tensor_reduce(nmz[:, 0:1], front.at(F_Z)[0:H, 0:N], AX.X, ALU.max,
                                            negate=True).then_inc(nmz_ready.sem, 1)
                    dve.wait_ge(zexp_ready.sem, zexp_ready.at(j, 1))
                    link(nc.vector.reciprocal(zrec[:, :], zsum[:, :]))
                    nc.vector.tensor_scalar(zexp[:, :], zexp[:, :], zrec[:, 0:1], 1.0 / N, ALU.mult,
                                            ALU.mult).then_inc(free, 1)
                elif step == "zt":
                    front.filled(dve, j, F_ZT)
                    nc.vector.tensor_copy(vz[:, :, C:C + H], front.at(F_ZT)[0:P, 0:T * H]
                                          .rearrange("p (t h) -> p t h", t=T)).then_inc(free, 1)
                elif step == "dft":
                    vr, vi = (front.at(F_DFT + s)[0:FW].rearrange("p (f c) -> p f c", f=2) for s in range(2))
                    front.filled(dve, j, F_DFT)
                    link(nc.vector.tensor_copy(zf[:, 0, :, :], vr[:, :, C:C + H]))
                    front.filled(dve, j, F_DFT + 1)
                    link(nc.vector.tensor_copy(zf[:, 1, :, :], vi[:, :, C:C + H]))

                    def times(dst, v, part):
                        for f in range(2):
                            done = nc.vector.tensor_tensor(
                                dst[:, f, :].rearrange("p (h d) -> p h d", d=D),
                                v[:, f, 0:C].rearrange("p (h d) -> p h d", d=D),
                                zf[:, part, f, :].rearrange("p (h a) -> p h a", a=1).broadcast_to([FW, H, D]), ALU.mult)
                        return done

                    times(ta, vr, 0)
                    link(times(tb, vi, 1))
                    link(nc.vector.tensor_tensor(of[:, 0], ta[:, :, :], tb[:, :, :], ALU.add))
                    times(ta, vi, 0).then_inc(free, 1)
                    times(tb, vr, 1).then_inc(free, 1)
                    front.emptied(dve, j, F_DFT + 1)
                    nc.vector.tensor_tensor(of[:, 1], ta[:, :, :], tb[:, :, :], ALU.subtract).then_inc(of_ready.sem, 1)
                elif step == "proj":
                    dve.wait_ge(hb_ready.sem, hb_ready.at(j, 1))
                    residual(front, j, F_PROJ, h, hb)
                    layernorm(h, xn, 1e-5, ln_done)
                elif step == "out":
                    residual(front, j, F_OUT, h, h)
                    layernorm(h, xn, 1e-5, ln_done)
                elif step == "qk":
                    rests(one, front, j, F_QK)

            def normalise(att, i):
                ring, u = att.ring, att.den
                for q in range(GROUPS):
                    ring.filled(dve, i, u + q)
                    if q:
                        dve.wait_ge(att.normed.sem, att.normed.at(i, q))
                    nc.vector.reciprocal(rc[:, :], ring.at(u + q)[:, 0:N]).then_inc(ring.free["dve"].sem, 1)
                    ring.emptied(dve, i, u + q)
                    nc.vector.tensor_tensor(av[:, q, :], av[:, q, :], rc[:, :], ALU.mult).then_inc(att.normed.sem, 1)

            def attention_step(att, i, slot):
                ring = att.ring
                n = 3 * att.kt if slot == "end" else slot
                if isinstance(n, int) and n and n % att.kt == 0:
                    q = n // att.kt - 1
                    dve.wait_ge(att.summed.sem, att.summed.at(i, 4 * n))
                    nc.vector.tensor_copy(av[:, q, :], aps[:, 0:N]).then_inc(att.copied.sem, 1)
                w = max_units(att, slot)
                if not w:
                    return
                q, units, complete = w
                for n in units:
                    hd, t, s = n // (T * att.halves), n // att.halves % T, n % att.halves
                    u = q * (att.mu + 1) + n
                    ring.filled(dve, i, u)
                    nc.vector.tensor_reduce(mxh[:, hd, t, s:s + 1], ring.at(u)[0:P, 0:att.width], AX.X, ALU.max,
                                            negate=att.halves == 1).then_inc(ring.free["dve"].sem, 1)
                if not complete:
                    return
                ring.emptied(dve, i, u)
                src = [mxh[:, :, :, s].rearrange("p h t -> p t h") for s in range(2)]
                if att.halves == 2:
                    link(nc.vector.tensor_tensor(mr[:, :, :], src[0], src[1], ALU.max))
                    link(nc.vector.tensor_scalar(mx[:, :, :], mr[:, :, :], -1.0, None, ALU.mult))
                else:
                    link(nc.vector.tensor_copy(mx[:, :, :], src[0]))
                link(nc.vector.tensor_copy(mp[:, :, 0, :], mx[:, :, :]))
                link(nc.vector.tensor_tensor(mr[:, :, :], mx[:, :, :], mp[:, :, 0, :], ALU.subtract))
                link(nc.vector.tensor_copy(mp[:, :, 1, :], mr[:, :, :]))
                nc.vector.tensor_tensor(mp[:, :, 2, :], mr[:, :, :], mp[:, :, 1, :], ALU.subtract).then_inc(att.maxed.sem, 1)

            def first_loop(i, with_front):
                restart()
                for slot in attention_slots(one):
                    attention_step(one, i, slot)
                    if with_front:
                        for step in FRONT.get(slot, ()):
                            front_step(i + 1, step)
                normalise(one, i)
                dve.wait_ge(hab_ready.sem, hab_ready.at(i, 1))
                dve.wait_ge(hx_ready.sem, hx_ready.at(i, 0))
                residual(back, i, R_PROJ, ha, hab)
                layernorm(ha, xna, 1e-5, lna_done)
                dve.wait_ge(lna_done.sem, lna_done.at(i, 1))
                layernorm(xna, xn5, 1e-6, lna_done)
                back.filled(dve, i, R_LOG)
                lgp = back.at(R_LOG)[0:P, 0:T * E].rearrange("p (t e) -> p t e", t=T)
                link(nc.vector.tensor_reduce(lmx[:, :], lgp, AX.X, ALU.max))
                for t in range(T):
                    done = nc.vector.tensor_scalar(lg[:, t, :], lgp[:, t, :], lmx[:, t:t + 1], None, ALU.subtract)
                done.then_inc(back.free["dve"].sem, 1)
                dve.wait_ge(lg_ready.sem, lg_ready.at(i, 0))
                nc.vector.tensor_copy(nta[:, :], lmx[:, :]).then_inc(lg_ready.sem, 1)
                dve.wait_ge(pe_ready.sem, pe_ready.at(i, 1))
                link(nc.vector.tensor_reduce(lmx[:, :], pr[:, :, :], AX.X, ALU.add))
                link(nc.vector.reciprocal(nta[:, :], lmx[:, :]))
                for t in range(T):
                    done = nc.vector.tensor_scalar(pr[:, t, :], pr[:, t, :], nta[:, t:t + 1], None, ALU.mult)
                done.then_inc(pr_ready.sem, 1)
                back.filled(dve, i, R_PRT)
                dve.wait_ge(spilled.sem, spilled.at(i, 0))
                nc.vector.tensor_copy(prT[:, :], back.at(R_PRT)[0:E, 0:N]).then_inc(back.free["dve"].sem, 1)

            for step in FRONT_ALL:
                front_step(0, step)
            with dve.Fori(0, B - 1) as i:
                first_loop(i, True)
            first_loop(B - 1, False)

            restart()
            nc.vector.memset(work[:, N:], 2.0)
            dve.wait_ge(picks_in.sem, 16)
            link(nc.vector.tensor_copy(work[:, 0:N], pall[:, :]))
            for _ in range(ROUNDS):
                link(nc.vector.max(top8[:, :], work[:, :]))
                link(nc.vector.match_replace(work[:, :], top8[:, :], work[:, :], -1.0))
            nc.vector.tensor_scalar(selall[:, :], work[:, 0:N], 0.0, None, ALU.is_lt).then_inc(picked.sem, 1)
            dve.wait_ge(picked.sem, 1)
            nc.vector.tensor_tensor(gateall[:, :], selall[:, :], pall[:, :], ALU.mult).then_inc(picked.sem, 1)

            def moe_step(j, step):
                if step == "count":
                    dve.wait_ge(moe_in.sem, moe_in.at(j, 32))
                    for k in range(2):
                        moe.filled(dve, j, M_CNT + k)
                        nc.vector.tensor_tensor(yT[:, k, :], yT[:, k, :], moe.at(k)[0:KC, 0:N],
                                                ALU.mult).then_inc(moe.free["dve"].sem, 1)
                elif step == "qk":
                    rests(two, moe, j, M_QK)

            def out_step(i, k):
                moe_out.filled(dve, i, k)
                for t in range(2 - k):
                    done = nc.vector.tensor_tensor(acc[:, 2 * k + t, :], tiles2(moe_out.at(k))[0:P, t, :], b_2[:, 0, :], ALU.add)
                done.then_inc(moe_out.free["dve"].sem, 1)

            def second_loop(i, with_moe):
                restart()
                for slot in attention_slots(two):
                    attention_step(two, i, slot)
                    for step in MOE.get(slot, ()):
                        if step in ("out0", "out1"):
                            out_step(i, int(step[3]))
                        elif with_moe:
                            moe_step(i + 1, step)
                normalise(two, i)
                residual(last, i, O_PROJ, acc, acc)
                last.emptied(dve, i, O_GATE + 1)
                dve.wait_ge(tail_in.sem, tail_in.at(i, 32))
                dve.wait_ge(stored.sem, stored.at(i, 0))
                link(nc.vector.tensor_tensor(fin[:, :, :], acc[:, :, :], gm[:, :, :], ALU.mult))
                nc.vector.tensor_tensor(fin[:, :, :], fin[:, :, :], hxb[:, :, :], ALU.add).then_inc(fin_ready.sem, 1)

            for step in MOE_ALL:
                moe_step(0, step)
            with dve.Fori(0, B - 1) as i:
                second_loop(i, True)
            second_loop(B - 1, False)

        @block.tensor
        def _(pe):
            mm = nc.tensor.matmul
            pe.wait_ge(loads.sem, 16 * NLOAD)
            pe.wait_ge(setup_dve.sem, 4)
            for m in range(2):
                for k in range(2):
                    done = mm(lin[0:KC, m, 0:SC], w_qkv[:, k, C + m * KC:C + (m + 1) * KC], xS[:, k, N:NK1],
                              start=k == 0, stop=k == 1)
                done.then_inc(setup_pe.sem, 1)
            for k in range(2):
                done = mm(mps[0:TK1, 0, 0:C], xS[:, k, (KT1 - 1) * TK1:NK1], w_qkv[:, k, 2 * C:], start=k == 0, stop=k == 1)
            done.then_inc(setup_pe.sem, 1)
            pe.wait_ge(setup_act.sem, 1)
            pe.wait_ge(sc_rest.sem, 2)
            pe.wait_ge(sc_pack.sem, 16 * 6)

            def transposes(ring, j, u, src, signals, k):
                pe.wait_ge(signals.sem, signals.at(j, k))
                for c in range(2):
                    b = ring.bank(pe, j, u + c)
                    for t in range(T):
                        done = nc.tensor.transpose(b[0:KC, t * P:(t + 1) * P],
                                                   src[:, t, c * KC:(c + 1) * KC], ident[0:P, 0:P])
                    done.then_inc(ring.full.sem, 1)

            def by_token(ring, j, u, acts, weights, rows, nt, first=0):
                for t in range(2 * first, nt):
                    if t % 2 == 0:
                        b = ring.bank(pe, j, u + t // 2)
                    for k, (x, w) in enumerate(zip(acts, weights)):
                        done = mm(tiles2(b)[0:rows, t % 2, :], x[:, t * rows:(t + 1) * rows], w,
                                  start=k == 0, stop=k == len(acts) - 1)
                    if t % 2 == 1 or t == nt - 1:
                        done.then_inc(ring.full.sem, 1)

            def hidden(ring, j, u, x, w, bias):
                for f in range(FT):
                    b = ring.bank(pe, j, u + f)
                    for k in range(2):
                        done = mm(b[:, 0:N], w[:, k, f * 128:(f + 1) * 128], x[:, k, 0:N],
                                  start=k == 0, stop=k == 1 and not bias)
                    if bias:
                        done = mm(b[:, 0:N], b_1[:, f * 128:(f + 1) * 128], sel[:, :], start=False, stop=True)
                    done.then_inc(ring.full.sem, 1)

            def queries_keys(ring, j, u, x, w, c0, bias):
                for m in range(4):
                    b = ring.bank(pe, j, u + m)
                    c = c0 + m * KC
                    for k in range(2):
                        done = mm(b[0:KC, 0:N], w[:, k, c:c + KC], x[:, k, 0:N],
                                  start=k == 0, stop=k == 1 and not bias)
                    if bias:
                        done = mm(b[0:KC, 0:N], b_1[:, c:c + KC], sel[:, :], start=False, stop=True)
                    done.then_inc(ring.full.sem, 1)

            def attention_step(att, i, slot):
                ring, kt, rows = att.ring, att.kt, att.rows
                if slot == "max0":
                    pe.wait_ge(att.pack_in.sem, att.pack_in.at(i, 192))
                n4 = GROUPS * kt if slot == "end" else slot
                if isinstance(n4, int):
                    if n4 < GROUPS * kt:
                        q, k = divmod(n4, kt)
                        if k == 0:
                            pe.wait_ge(att.rows_in.sem, att.rows_in.at(i, 48 * (q + 1)))
                        for n in range(4 * n4, 4 * n4 + 4):
                            pe.wait_ge(att.exped.sem, att.exped.at(i, n - 2))
                            mm(sps[0:rows, n % 3, 0:N], kpack[:, 4 * q + n % 4, k * rows:(k + 1) * rows],
                               qpack[:, 4 * q + n % 4, :], start=True, stop=True).then_inc(att.scored.sem, 1)
                    if n4 > 0:
                        q, k = divmod(n4 - 1, kt)
                        if k == 0:
                            pe.wait_ge(att.copied.sem, att.copied.at(i, q))
                        for n in range(4 * n4 - 4, 4 * n4):
                            j = n % 4
                            pe.wait_ge(att.exped.sem, att.exped.at(i, n + 1))
                            mm(aps[32 * j:32 * j + 32, 0:N], att.values[:, k, 4 * q + j, :], prob[0:rows, n % NP, :],
                               start=k == 0, stop=k == kt - 1).then_inc(att.summed.sem, 1)
                w = max_units(att, slot)
                if not w:
                    return
                q, units, complete = w
                for n in units:
                    hd, t, s = n // (T * att.halves), n // att.halves % T, n % att.halves
                    b = ring.bank(pe, i, q * (att.mu + 1) + n)
                    mm(b[0:P, 0:att.width], qpack[0:6 * D, 4 * q + hd, t * P:(t + 1) * P],
                       kpack[0:6 * D, 4 * q + hd, s * att.width:(s + 1) * att.width],
                       start=True, stop=True).then_inc(ring.full.sem, 1)

            def max_transposed(att, i, slot):
                w = max_units(att, slot)
                if not w or not w[2]:
                    return
                b = att.ring.bank(pe, i, (w[0] + 1) * (att.mu + 1) - 1)
                pe.wait_ge(att.maxed.sem, att.maxed.at(i, w[0] + 1))
                pe.sem_inc(gate_pe.sem)
                for t in range(T):
                    done = nc.tensor.transpose(b[0:12, t * (P // 2):(t + 1) * (P // 2)].bitcast(bf16),
                                               mp[:, t].rearrange("p s h -> p (s h)"), identb[0:P, 0:P])
                done.then_inc(att.ring.full.sem, 1)

            def denominators(att, i):
                for q in range(GROUPS):
                    b = att.ring.bank(pe, i, att.den + q)
                    pe.wait_ge(att.copied.sem, att.copied.at(i, q + 1))
                    mm(b[:, 0:N], spread[:, :], av[:, q, :], start=True, stop=True).then_inc(att.ring.full.sem, 1)

            def front_step(j, step):
                if step == "tok":
                    pe.wait_ge(x_in.sem, x_in.at(j, 48))
                    b = front.bank(pe, j, F_TOK)
                    for t, rows in ((0, P), (1, IMG - P)):
                        for k in range(2):
                            done = mm(tiles2(b)[0:rows, t, :], pT[:, k, t * P:t * P + rows], w_tok[:, k, :],
                                      start=k == 0, stop=k == 1)
                    done.then_inc(front.full.sem, 1)
                elif step == "t1":
                    transposes(front, j, F_T1, xn, ln_done, 1)
                elif step == "zv":
                    front.emptied(pe, j, F_T1 + 1)
                    b = front.bank(pe, j, F_Z)
                    for k in range(2):
                        done = mm(b[0:H, 0:N], w_a[:, k, :], xT[:, k, :], start=k == 0, stop=k == 1)
                    done.then_inc(front.full.sem, 1)
                    by_token(front, j, F_V, [xT[:, k, :] for k in range(2)], [w_v0[:, k, :] for k in range(2)], P, T)
                elif step == "zt":
                    b = front.bank(pe, j, F_ZT)
                    front.emptied(pe, j, F_Z)
                    pe.sem_inc(gate_pe.sem)
                    for t in range(T):
                        done = nc.tensor.transpose(b[0:P, t * H:(t + 1) * H], zexp[:, t * P:(t + 1) * P], ident[0:H, 0:H])
                    done.then_inc(front.full.sem, 1)
                elif step == "dft":
                    for part in range(2):
                        b = front.bank(pe, j, F_DFT + part)
                        front.emptied(pe, j, F_ZT)
                        for f in range(2):
                            for t in range(T):
                                done = mm(b[0:FW, 256 * f:256 * f + C + H], dft[:, t, part, f, :], vz[:, t, :],
                                          start=t == 0, stop=t == T - 1)
                        done.then_inc(front.full.sem, 1)
                elif step == "inv":
                    pe.wait_ge(of_ready.sem, of_ready.at(j, 1))
                    for m in range(2):
                        b = front.bank(pe, j, F_INV + m)
                        for n in range(4):
                            done = mm(b[0:KC, 0:N], of[:, n // 2, n % 2, m * KC:(m + 1) * KC], idft[:, n // 2, n % 2, :],
                                      start=n == 0, stop=n == 3)
                        done.then_inc(front.full.sem, 1)
                elif step == "proj":
                    front.emptied(pe, j, F_INV + 1)
                    by_token(front, j, F_PROJ, [aT[:, k, :] for k in range(2)], [w_p0[:, k, :] for k in range(2)], P, T)
                elif step == "t2":
                    transposes(front, j, F_T2, xn, ln_done, 2)
                elif step == "hidden":
                    front.emptied(pe, j, F_T2 + 1)
                    hidden(front, j, F_HID, xT, w_in, False)
                elif step == "out":
                    front.emptied(pe, j, F_HID + FT - 1)
                    by_token(front, j, F_OUT, [g[:, k, :] for k in range(FT)], [w_out[:, k, :] for k in range(FT)], P, T)
                elif step == "t3":
                    transposes(front, j, F_T3, xn, ln_done, 3)
                elif step == "qk":
                    front.emptied(pe, j, F_T3 + 1)
                    queries_keys(front, j, F_QK, xS, w_qkv, 0, False)
                elif step == "values":
                    by_token(front, j, F_VAL, [xS[:, k, :] for k in range(2)], [w_qkv[:, k, 2 * C:] for k in range(2)], TK1, 4)

            def first_loop(i, with_front):
                front.emptied(pe, i, F_VAL + 1)
                for slot in attention_slots(one):
                    attention_step(one, i, slot)
                    if with_front:
                        for step in FRONT.get(slot, ()):
                            front_step(i + 1, step)
                    max_transposed(one, i, slot)
                denominators(one, i)
                pe.wait_ge(one.normed.sem, one.normed.at(i, GROUPS))
                by_token(back, i, R_PROJ, [av[:, k, :] for k in range(GROUPS)], [w_p1[:, k, :] for k in range(GROUPS)], P, T)
                transposes(back, i, R_T4, xna, lna_done, 1)
                back.emptied(pe, i, R_T4 + 1)
                b = back.bank(pe, i, R_LOG)
                for t in range(T):
                    for k in range(2):
                        done = mm(b[0:P, t * E:(t + 1) * E], xTa[:, k, t * P:(t + 1) * P], w_r[:, k, :],
                                  start=k == 0, stop=k == 1)
                done.then_inc(back.full.sem, 1)
                b = back.bank(pe, i, R_PRT)
                pe.wait_ge(pr_ready.sem, pr_ready.at(i, 1))
                for t in range(T):
                    done = nc.tensor.transpose(b[0:E, t * P:(t + 1) * P], pr[:, t, :], ident[0:P, 0:P])
                done.then_inc(back.full.sem, 1)
                transposes(back, i, R_T5, xn5, lna_done, 2)

            for step in FRONT_ALL:
                front_step(0, step)
            with pe.Fori(0, B - 1) as i:
                first_loop(i, True)
            first_loop(B - 1, False)

            def moe_step(j, step):
                if step == "count":
                    pe.wait_ge(moe_in.sem, moe_in.at(j, 32))
                    moe_out.emptied(pe, j - 1, 1)
                    for m in range(2):
                        b = moe.bank(pe, j, M_CNT + m)
                        mm(b[0:KC, 0:N], emask[:, m * KC:(m + 1) * KC], sel[:, :], start=True, stop=True).then_inc(moe.full.sem, 1)
                elif step == "hidden":
                    moe.emptied(pe, j, M_CNT + 1)
                    hidden(moe, j, M_HID, yT, w_1, True)
                elif step == "qk":
                    queries_keys(moe, j, M_QK, yT, w_1, FH, True)
                elif step == "values":
                    by_token(moe, j, M_VAL, [yT[:, k, :] for k in range(2)] + [sel[:, :]],
                             [w_1[:, k, FH + 2 * C:] for k in range(2)] + [b_1[:, FH + 2 * C:]], P, T)

            def out_step(i, k):
                if k == 0:
                    moe.emptied(pe, i, M_VAL + 1)
                    moe.emptied(pe, i, M_QK + 3)
                    moe.emptied(pe, i, M_HID + FT - 1)
                by_token(moe_out, i, 0, [g[:, f, :] for f in range(FT)], [w_2[:, 0, f, :] for f in range(FT)],
                         P, T if k else 2, first=k)

            def second_loop(i, with_moe):
                for slot in attention_slots(two):
                    attention_step(two, i, slot)
                    for step in MOE.get(slot, ()):
                        if step in ("out0", "out1"):
                            out_step(i, int(step[3]))
                        elif with_moe:
                            moe_step(i + 1, step)
                    max_transposed(two, i, slot)
                denominators(two, i)
                pe.wait_ge(tail_in.sem, tail_in.at(i, 32))
                by_token(last, i, O_GATE, [gate[:, :]], [emask[:, :]], P, T)
                pe.wait_ge(two.normed.sem, two.normed.at(i, GROUPS))
                by_token(last, i, O_PROJ, [av[:, k, :] for k in range(GROUPS)],
                         [w_2a[:, 0, k, :] for k in range(GROUPS)], P, T)

            for step in MOE_ALL:
                moe_step(0, step)
            with pe.Fori(0, B - 1) as i:
                second_loop(i, True)
            second_loop(B - 1, False)


def kernel(**inputs):
    import numpy as _np
    import concourse.bacc as _bacc
    from concourse import mybir as _mybir
    from concourse.bass_utils import run_bass_kernel_spmd as _run

    a = {k: _np.asarray(v) for k, v in inputs.items()}

    def rows(w, r):
        return w.reshape(-1, r, w.shape[1]).transpose(1, 0, 2)

    nh = a["x"].shape[2] // 16
    k = _np.minimum(_np.arange(2 * FW), NF)
    live = (_np.arange(2 * FW) < NF)[:, None]
    ang = 2 * _np.pi * ((k[:, None] * _np.arange(N)[None, :]) % N) / N
    both = _np.stack([_np.cos(ang) * live, _np.sin(ang) * live * ((k % (N // 2)) != 0)[:, None]])
    weight = _np.where((k % (N // 2)) == 0, 1.0, 2.0)[:, None]
    dft = both.reshape(2, 2, FW, T, P).transpose(4, 3, 0, 1, 2)
    idft = (both * weight / N).reshape(2, 2, FW, N).transpose(2, 0, 1, 3)
    width = C // 2 ** (E - 1 - _np.arange(E))
    emask = (_np.arange(C)[None, :] < width[:, None])
    spread = _np.zeros((128, 128))
    for m in range(128):
        spread[32 * (m // 32) + D, m] = 1.0
    arrays = {
        "x": a["x"].reshape(B, nh, 16, nh, 16).transpose(0, 2, 4, 1, 3).reshape(B, 2, 128, IMG).transpose(0, 2, 1, 3),
        "txt": a["txt"],
        "w_tok": rows(a["L0_tok_W"].T, 128),
        "w_a": rows(a["L0_attn_W_A"], KC),
        "w_v0": rows(a["L0_attn_W_V"], KC),
        "w_p0": rows(a["L0_attn_W_proj"], KC),
        "b_p0": a["L0_attn_b_proj"],
        "w_in": rows(a["L0_ffn_in_weight"].T, KC),
        "b_in": a["L0_ffn_in_bias"].reshape(FT, 128).T,
        "w_out": rows(a["L0_ffn_out_weight"], 128),
        "sc": rows(a["L1_attn_sc_token"][0].T, KC),
        "w_qkv": rows(a["L1_attn_W_qkv"], KC),
        "w_p1": a["L1_attn_W_proj"],
        "b_p1": a["L1_attn_b_proj"],
        "w_r": rows(a["L1_ffn_w_router"].T, KC),
        "gamma": a["L1_ffn_gamma1"].reshape(2, KC).T,
        "beta": a["L1_ffn_beta1"].reshape(2, KC).T,
        "w_1": rows(a["L1_ffn_w1"].T, KC),
        "b_1": a["L1_ffn_b1"].reshape(1, -1),
        "w_2": a["L1_ffn_w2"][:, :FH].reshape(2, C, FT, 128).transpose(3, 0, 2, 1),
        "w_2a": a["L1_ffn_w2"][:, FH:].reshape(2, C, C).transpose(0, 2, 1),
        "b_2": a["L1_ffn_b2"].reshape(2, C),
        "ident": _np.eye(128, dtype=_np.float32),
        "dft": dft.astype(_np.float32),
        "idft": idft.astype(_np.float32),
        "spread": spread.astype(_np.float32),
        "emask": emask.astype(_np.float32),
    }
    nc = _bacc.Bacc("TRN2", target_bir_lowering=False, num_devices=1)
    ins, aps = {}, {}
    for name, v in arrays.items():
        v = _np.ascontiguousarray(v)
        ins[f"in_{name}"] = v
        aps[name] = nc.dram_tensor(f"in_{name}", v.shape, _mybir.dt.from_np(v.dtype), kind="ExternalInput").ap()
    aps["out"] = nc.dram_tensor("out_0", (B, N, C), _mybir.dt.float32, kind="ExternalOutput").ap()
    build(nc, aps)
    r = _run(nc, [ins], core_ids=[0])
    return r.results[0]["out_0"]
```

```python
import numpy as np
import concourse.bass as bass
from concourse import mybir
from contextlib import ExitStack

B = 16
IMG, TXT, SC = 196, 128, 196
N = IMG + TXT
C = 192
P, T = 108, 3
KC = 96
KP = 128
H, D = 12, 16
NK1 = N + SC
TK1, KT1 = 104, 5
TK2, KT2 = P, T
FH = 768
FT = FH // 128
E, CAP = 4, N // 2
PAD = 8 * ((CAP + 7) // 8) - CAP
ROUNDS = (CAP + PAD) // 8
NF = N // 2 + 1
FW = 82
SCALE = float(D) ** -0.5
Q_PARTS = (0, 0, 0, 1, 1, 2)
K_PARTS = (0, 1, 2, 0, 1, 0)
GROUPS = 3


class Ring:

    def __init__(self, name, banks, fillings, signal, first):
        self.banks, self.uses, self.start, self.size = banks, [], {}, {}
        for step, uses in fillings:
            self.start[step], self.size[step] = len(self.uses), len(uses)
            self.uses += uses
        self.full = signal(name + "_full", len(self.uses), first=first)
        self.free = {e: signal(f"{name}_free_{e}", self.uses.count(e), first=first) for e in sorted(set(self.uses))}

    def skip(self, eng, who, i, step):
        if step not in self.start:
            return
        u, n = self.start[step], self.size[step]
        if who == "pe":
            if u < 2:
                for v in (1, 2):
                    self.emptied(eng, i - 1, len(self.uses) - v)
            for v in range(max(u - 2, 0), u):
                self.emptied(eng, i, v)
            eng.wait_ge(self.full.sem, self.full.at(i, u))
            eng.sem_inc(self.full.sem, n)
        elif self.uses[u:u + n].count(who):
            s = self.free[who]
            eng.wait_ge(s.sem, s.at(i, self.uses[:u].count(who)))
            eng.sem_inc(s.sem, self.uses[u:u + n].count(who))

    def order(self, u):
        return self.uses[:u + 1].count(self.uses[u])

    def filled(self, eng, i, u):
        eng.wait_ge(self.full.sem, self.full.at(i, u + 1))

    def emptied(self, eng, i, u):
        s = self.free[self.uses[u]]
        eng.wait_ge(s.sem, s.at(i, self.order(u)))

    def bank(self, eng, i, u):
        if u >= 2:
            self.emptied(eng, i, u - 2)
        else:
            p = len(self.uses) - 1
            while p % 2 != u % 2:
                p -= 1
            self.emptied(eng, i - 1, p)
        return self.banks[:, u % 2, :]

    def at(self, u):
        return self.banks[:, u % 2, :]


class Signal:

    def __init__(self, sem, per, primed=1, first=0):
        self.sem, self.per, self.primed, self.first = sem, per, primed, first

    def at(self, i, n):
        return (i + self.primed) * self.per + n


def build(nc, A):
    fp32, bf16, i32 = mybir.dt.float32, mybir.dt.bfloat16, mybir.dt.int32
    ALU, ACT, AX = mybir.AluOpType, mybir.ActivationFunctionType, mybir.AxisListType
    ctx = ExitStack()
    with ctx:
        def sb(name, shape, dt=fp32):
            return ctx.enter_context(nc.sbuf_tensor(name, shape, dt))

        primed = []

        def signal(name, per=1, prime=1, first=0):
            s = Signal(ctx.enter_context(nc.semaphore(name)), per, prime - first, first)
            if per and prime:
                primed.append(s)
            return s

        w_tok = sb("w_tok", [128, 2, C])
        w_a = sb("w_a", [KP, 2, H])
        w_v0 = sb("w_v0", [KP, 2, C])
        w_p0 = sb("w_p0", [KP, 2, C])
        b_p0 = sb("b_p0", [P, C])
        w_in = sb("w_in", [KP, 2, FH])
        b_in = sb("b_in", [128, FT])
        w_out = sb("w_out", [128, FT, C])
        w_qkv = sb("w_qkv", [KP, 2, 3 * C])
        w_p1 = sb("w_p1", [128, GROUPS, C])
        b_p1 = sb("b_p1", [P, C])
        w_r = sb("w_r", [KC, 2, E])
        gamma = sb("gamma", [KC, 2])
        beta = sb("beta", [KC, 2])
        w_1 = sb("w_1", [KP, 2, FH + 3 * C])
        w_2 = sb("w_2", [128, 2, FT, C])
        w_2a = sb("w_2a", [128, 2, GROUPS, C])
        b_2 = sb("b_2", [P, 2, C])
        ident = sb("ident", [128, 128])
        identb = sb("identb", [128, 128], bf16)
        dft = sb("dft", [KP, T, 2, 2, FW])
        idft = sb("idft", [KP, 2, 2, N])
        rc = sb("rc", [KP, N])
        gather = sb("gather", [128, GROUPS, H])
        spread = sb("spread", [KP, GROUPS, 128])
        emask = sb("emask", [KP, 2 * KP])
        emaskc = sb("emaskc", [KP, C])

        pT = sb("pT", [128, 2, IMG])
        hin = sb("hin", [P, T, C])
        hb = sb("hb", [P, T, C])
        h = sb("h", [P, T, C])
        xn = sb("xn", [P, T, C])
        st = sb("st", [P, T, 6])
        mv = sb("mv", [P, T, 2])
        var = sb("var", [P, T])
        rs = sb("rs", [P, T])
        nt = sb("nt", [P, T])
        xT = sb("xT", [KP, 2, N])
        xS = sb("xS", [KP, 2, NK1])
        nmz = sb("nmz", [H, 1])
        zsum = sb("zsum", [H, 1])
        zrec = sb("zrec", [H, 1])
        zexp = sb("zexp", [H, N])
        vz = sb("vz", [KP, T, C + H])
        zf = sb("zf", [FW, 2, 2, H])
        ta = sb("ta", [FW, 2, C])
        tb = sb("tb", [FW, 2, C])
        of = sb("of", [KP, 2, 2, C])
        aT = sb("aT", [KP, 2, N])
        g = sb("g", [128, FT, N])
        piece = sb("piece", [KC, 4, 3, N], bf16)
        rest = sb("rest", [KC, 4, N])
        qpack = sb("qpack", [KP, H, N], bf16)
        kpack = sb("kpack", [KP, H, NK1], bf16)
        v1 = sb("v1", [KP, KT1, H, 32])
        v2 = sb("v2", [KP, KT2, H, 32])
        mxh = sb("mxh", [P, 4, T, 2])
        mx = sb("mx", [P, T, 4])
        mr = sb("mr", [P, T, 4])
        mp = sb("mp", [P, T, 3, 4], bf16)
        mT = sb("mT", [12, N], bf16)
        NP = 12
        prob = sb("prob", [128, NP, N])
        av = sb("av", [128, GROUPS, N])
        ha = sb("ha", [P, T, C])
        hc = sb("hc", [P, T, C])
        hab = sb("hab", [P, T, C])
        xna = sb("xna", [P, T, C])
        xn5 = sb("xn5", [P, T, C])
        xTa = sb("xTa", [KC, 2, N])
        lg = sb("lg", [P, T, E])
        lmx = sb("lmx", [P, T])
        nta = sb("nta", [P, T])
        pr = sb("pr", [P, T, E])
        prT = sb("prT", [E, N])
        hx = sb("hx", [P, T, C])
        yA = sb("yA", [KP, 2, N])
        pall = sb("pall", [B * E, N])
        work = sb("work", [B * E, N + PAD])
        top8 = sb("top8", [B * E, 8])
        selall = sb("selall", [B * E, N])
        gateall = sb("gateall", [B * E, N])
        sel = sb("sel", [KP, N])
        gate = sb("gate", [KP, N])
        yT = sb("yT", [KP, 2, N])
        gm = sb("gm", [P, T, C])
        acc = sb("acc", [P, T, C])
        hxb = sb("hxb", [P, T, C])
        fin = sb("fin", [P, T, C])

        lin = ctx.enter_context(nc.psum_tensor("lin", [128, 2, 512], fp32))
        mps = ctx.enter_context(nc.psum_tensor("mps", [128, 2, 512], fp32))
        sps = ctx.enter_context(nc.psum_tensor("sps", [128, 3, 512], fp32))
        aps = ctx.enter_context(nc.psum_tensor("aps", [128, 512], fp32))

        def dram(name, shape, dt=fp32):
            return nc.dram_tensor(name, shape, dt, kind="Internal").ap()

        scr = dram("scr", (2, 3, C, N), bf16)
        hx_d = dram("hx_d", (B, P, T, C))
        y_d = dram("y_d", (B, KP, 2, N))
        pr_d = dram("pr_d", (B * E, N))
        sel_d = dram("sel_d", (B, E, N))
        gate_d = dram("gate_d", (B, E, N))

        TAIL = {0: ["den"], 1: ["norm"], 2: ["proj4", "ln5"], 4: ["t4"], 5: ["log"], 6: ["exp"], 7: ["prob"], 8: ["prt", "t5"]}
        LATE = {0: ["t2"], 2: ["hidden"], 3: ["out"], 5: ["t3"], 6: ["qk"], "end": ["values"]}
        EARLY = {8: ["tok"], 10: ["t1"], 11: ["zv"], 12: ["zt"], 13: ["dft"], 14: ["inv"], "end": ["proj"]}
        TAIL2 = {0: ["den"], 1: ["norm"], 2: ["gate", "final"]}
        MOE = {0: ["count"], 1: ["qk"], 5: ["hidden"], "end": ["values"]}
        OUT = {3: ["out"]}
        d, a = ["dve"], ["act"]
        BANKS = {"tok": a, "t1": a * 2, "zv": d + a * 2, "zt": d, "dft": d * 2, "inv": a * 2, "proj": d * 2, "t2": a * 2,
                 "hidden": a * 6, "out": d * 2, "t3": a * 2, "qk": d * 4, "values": a * 2,
                 "den": d, "norm": d * GROUPS, "proj4": d * 2, "t4": a * 2, "log": d, "prt": d, "t5": a * 2,
                 "gate": a * 2, "final": d * 2, "count": d * 2}

        def fillings(slots, streams, att=None):
            found = []
            for slot in slots:
                w = att.maxima(slot) if att else None
                if w:
                    found.append((("max", slot), d * len(w[1])))
                for stream in streams:
                    found += [(step, BANKS[step]) for step in stream.get(slot, ()) if step in BANKS]
                if w and w[2]:
                    found.append((("row", slot), a))
            return found

        class Attention:

            def __init__(self, name, kt, rows, halves, values, streams, first):
                self.kt, self.rows, self.halves, self.values = kt, rows, halves, values
                self.width = N if halves == 1 else NK1 // 2
                self.mu = 4 * T * halves
                self.units = H * kt
                self.slots = list(range(GROUPS * kt)) + ["end"]
                self.ring = Ring(name + "_mps", mps, fillings(self.slots, streams, self), signal, first)
                self.scored = signal(name + "_scored", self.units)
                self.exped = signal(name + "_exped", self.units)
                self.summed = signal(name + "_summed", self.units)
                self.copied = signal(name + "_copied", GROUPS)
                self.maxed = signal(name + "_maxed", GROUPS)
                self.rows_in = signal(name + "_rows_in", 48 * GROUPS)
                self.first = signal(name + "_first", 4)
                self.third = signal(name + "_third", 4)
                self.second = signal(name + "_second", 4)
                self.scr_in = signal(name + "_scr_in", 64)
                self.pack_in = [signal(f"{name}_pack_in{q}", 192) for q in range(GROUPS)]

            def maxima(self, slot):
                if slot == "end":
                    return None
                q, k = divmod(slot, self.kt)
                parts = self.kt - 1
                if k == parts:
                    return None
                size = self.mu // parts
                return (q + 1) % GROUPS, range(k * size, (k + 1) * size), k == parts - 1

            def batch(self, i, q):
                if q:
                    return i if has(i, 0, B - 1) else None
                return i + 1 if has(i, -1, B - 2) else None

        def has(i, lo, hi):
            return not isinstance(i, int) or lo <= i <= hi

        one = Attention("own_shared", KT1, TK1, 2, v1, [TAIL], -2)
        two = Attention("own", KT2, TK2, 1, v2, [TAIL2], -1)
        back, last = one.ring, two.ring
        front = Ring("front", lin, fillings(one.slots, [EARLY, LATE]), signal, -2)
        moe = Ring("moe", lin, fillings(two.slots, [OUT, MOE]), signal, -1)
        F, R, M, O = front.start, back.start, moe.start, last.start

        def streams_of(i, second):
            if second:
                return [(TAIL2, last, i - 1, has(i, 1, B)), (OUT, moe, i, has(i, 0, B - 1)),
                        (MOE, moe, i + 1, has(i, -1, B - 2))]
            return [(TAIL, back, i - 1, has(i, 1, B)), (EARLY, front, i + 2, has(i, -2, B - 3)),
                    (LATE, front, i + 1, has(i, -1, B - 2))]

        def iteration(eng, who, i, second, quad, maxima, rows, step):
            att = two if second else one
            for slot in att.slots:
                if has(i, 0, B - 1):
                    quad(att, i, slot)
                w = att.maxima(slot)
                b = att.batch(i, w[0]) if w else None
                if w and b is not None:
                    maxima(att, i, b, slot)
                elif w:
                    att.ring.skip(eng, who, i, ("max", slot))
                for steps, ring, j, present in streams_of(i, second):
                    for name in steps.get(slot, ()):
                        if present:
                            step(j, i, name)
                        else:
                            ring.skip(eng, who, i, name)
                if w and w[2] and b is not None:
                    rows(att, i, b, slot)
                elif w and w[2]:
                    att.ring.skip(eng, who, i, ("row", slot))

        def loops(eng, run, second):
            for i in range(-1 if second else -2, 1):
                run(i)
            with eng.Fori(1, B - 1 if second else B - 2) as i:
                run(i)
            for i in range(B - 1 if second else B - 2, B + 1):
                run(i)

        loads, setup_dve, setup_pe, setup_act, setup_pool, sc_first, sc_rest, sc_mid, sc_pieces, sc_scr, sc_pack = (
            signal(n, 0) for n in ("loads", "setup_dve", "setup_pe", "setup_act", "setup_pool", "sc_first",
                                   "sc_rest", "sc_mid", "sc_pieces", "sc_scr", "sc_pack"))
        x_in = signal("x_in", 48, prime=0)
        hb_ready = signal("hb_ready")
        hab_ready = signal("hab_ready")
        hc_ready = signal("hc_ready")
        ln_done = signal("ln_done", 3)
        lna_done = signal("lna_done", 2)
        nmz_ready = signal("nmz_ready")
        zexp_ready = signal("zexp_ready")
        of_ready = signal("of_ready")
        lg_ready = signal("lg_ready")
        pe_ready = signal("pe_ready")
        pr_ready = signal("pr_ready")
        hx_ready = signal("hx_ready")
        spilled = signal("spilled", 48)
        picks_in = signal("picks_in", 0)
        picked = signal("picked", 0)
        picks_out = signal("picks_out", 0)
        moe_in = signal("moe_in", 32)
        tail_in = signal("tail_in", 32)
        yT_ready = signal("yT_ready", 2)
        fin_ready = signal("fin_ready")
        stored = signal("stored", 16)
        dve_link = signal("dve_link", 0)
        gate_pe, gate_pool, gate_sp = signal("gate_pe", 0), signal("gate_pool", 0), signal("gate_sp", 0)

        SETUP_POOL, SETUP_DVE = 11, 13
        block = ctx.enter_context(nc.Block())

        LOADS = [
            (w_tok, A["w_tok"]), (w_a, A["w_a"]), (w_v0, A["w_v0"]), (w_p0, A["w_p0"]),
            (w_in, A["w_in"]), (b_in, A["b_in"]), (w_out, A["w_out"]), (w_qkv, A["w_qkv"]),
            (w_r, A["w_r"]), (gamma, A["gamma"]), (beta, A["beta"]), (w_1, A["w_1"]),
            (w_2, A["w_2"]), (ident, A["ident"]), (dft, A["dft"]), (idft, A["idft"]),
            (spread, A["spread"]), (gather, A["gather"]), (emask, A["emask2"]), (emaskc, A["emask"])]
        NLOAD = len(LOADS) + 3 * H + 3 + 1

        def tiles2(bank):
            return bank.rearrange("p (t c) -> p t c", t=2)[:, :, 0:C]

        @block.sync
        def _(sp):
            for s in primed:
                sp.sem_inc(s.sem, s.at(s.first, 0))
            for dst, src in LOADS:
                sp.dma_start(dst.ap(), src).then_inc(loads.sem, 16)
            sp.wait_ge(setup_pool.sem, 2)
            for hd in range(H):
                r = 32 * (hd % 4)
                sp.dma_start(w_p1[r:r + D, hd // 4, :], A["w_p1"][hd * D:(hd + 1) * D, :]).then_inc(loads.sem, 16)
                for s in range(2):
                    sp.dma_start(w_2a[r:r + D, s, hd // 4, :],
                                 A["w_2a"][s, hd * D:(hd + 1) * D, :]).then_inc(loads.sem, 16)
            sp.dma_start(b_p0[:, :], A["b_p0"].partition_broadcast(P)).then_inc(loads.sem, 16)
            sp.dma_start(b_p1[:, :], A["b_p1"].partition_broadcast(P)).then_inc(loads.sem, 16)
            sp.dma_start(b_2[:, :, :], A["b_2"].partition_broadcast(P)).then_inc(loads.sem, 16)
            sp.dma_start(xS[0:KC, :, N:NK1], A["sc"]).then_inc(loads.sem, 16)
            sp.wait_ge(setup_dve.sem, SETUP_DVE)
            sp.wait_ge(sc_pieces.sem, 2)
            for m in range(2):
                sp.dma_start(scr[1, :, m * KC:(m + 1) * KC, 0:SC].rearrange("s p n -> p s n"),
                             piece[:, 2 + m, :, 0:SC]).then_inc(sc_scr.sem, 16)
            sp.wait_ge(sc_scr.sem, 32)
            for r, s in enumerate(K_PARTS):
                sp.dma_start(kpack[r * D:(r + 1) * D, :, N:NK1],
                             scr[1, s, :, 0:SC].rearrange("(h d) n -> d h n", d=D)).then_inc(sc_pack.sem, 16)
            sp.wait_ge(sc_pack.sem, 16 * 6)

            def to_dram(att, j):
                sp.wait_ge(att.pack_in[-1].sem, att.pack_in[-1].at(j - 1, 192))
                for m in range(4):
                    sp.wait_ge(att.third.sem, att.third.at(j, m + 1))
                    sp.dma_start(scr[m // 2, :, (m % 2) * KC:(m % 2 + 1) * KC, :].rearrange("s p n -> p s n"),
                                 piece[:, m, :, :]).then_inc(att.scr_in.sem, 16)
                sp.wait_ge(att.scr_in.sem, att.scr_in.at(j, 64))
                sp.sem_inc(gate_sp.sem)

            def pack(att, j, q):
                sp.sem_inc(gate_sp.sem)
                sp.wait_ge(att.exped.sem, att.exped.at(j - 1, 4 * att.kt * (q + 1)))
                for r in range(6):
                    for side, dst, which in ((0, qpack, Q_PARTS[r]), (1, kpack, K_PARTS[r])):
                        sp.dma_start(dst[r * D:(r + 1) * D, 4 * q:4 * q + 4, 0:N],
                                     scr[side, which, 64 * q:64 * q + 64, :].rearrange("(h d) n -> d h n", d=D)
                                     ).then_inc(att.pack_in[q].sem, 16)

            def max_rows(att, i, slot):
                q = att.maxima(slot)[0]
                if att.batch(i, q) is None:
                    return
                att.ring.emptied(sp, i, att.ring.start["row", slot])
                for s in range(3):
                    sp.dma_start(qpack[6 * D + s:6 * D + s + 1, 4 * q:4 * q + 4, :],
                                 mT[4 * s:4 * s + 4, :]).then_inc(att.rows_in.sem, 16)

            def first_loop(i):
                j = i - 1
                max_rows(one, i, KT1 - 2)
                if has(i, 1, B):
                    sp.wait_ge(hx_ready.sem, hx_ready.at(j, 1))
                    sp.dma_start(hx_d[j], hx[:, :, :]).then_inc(spilled.sem, 16)
                if has(i, -1, B - 2):
                    to_dram(one, i + 1)
                max_rows(one, i, 2 * KT1 - 2)
                if has(i, -1, B - 2):
                    pack(one, i + 1, 0)
                    pack(one, i + 1, 1)
                if has(i, 1, B):
                    back.emptied(sp, i, R["prt"])
                    sp.sem_inc(gate_sp.sem)
                    sp.dma_start(pr_d[bass.ds(j * E, E), :], prT[:, :]).then_inc(spilled.sem, 16)
                    back.emptied(sp, i, R["t5"] + 1)
                    sp.dma_start(y_d[j], yA[:, :, :]).then_inc(spilled.sem, 16)
                max_rows(one, i, 3 * KT1 - 2)
                if has(i, -1, B - 2):
                    pack(one, i + 1, 2)

            loops(sp, first_loop, False)
            sp.wait_ge(spilled.sem, spilled.at(B - 1, 48))
            sp.dma_start(pall[:, :], pr_d[:, :]).then_inc(picks_in.sem, 16)
            sp.wait_ge(picked.sem, 2)
            sp.dma_start(sel_d.rearrange("b e n -> (b e) n"), selall[:, :]).then_inc(picks_out.sem, 16)
            sp.dma_start(gate_d.rearrange("b e n -> (b e) n"), gateall[:, :]).then_inc(picks_out.sem, 16)
            sp.wait_ge(picks_out.sem, 32)

            def second_loop(i):
                if has(i, -1, B - 2):
                    moe.filled(sp, i - 1, M["values"] + 1)
                    sp.dma_start(yT[:, :, :], y_d[i + 1]).then_inc(moe_in.sem, 16)
                    sp.dma_start(sel[0:E, :], sel_d[i + 1]).then_inc(moe_in.sem, 16)
                max_rows(two, i, KT2 - 2)
                if has(i, 1, B):
                    sp.wait_ge(fin_ready.sem, fin_ready.at(i - 1, 1))
                    sp.dma_start(A["out"][i - 1].rearrange("(t p) c -> p t c", p=P), fin[:, :, :]).then_inc(stored.sem, 16)
                if has(i, 0, B - 1):
                    sp.dma_start(gate[0:E, :], gate_d[i]).then_inc(tail_in.sem, 16)
                    sp.dma_start(hxb[:, :, :], hx_d[i]).then_inc(tail_in.sem, 16)
                if has(i, -1, B - 2):
                    to_dram(two, i + 1)
                max_rows(two, i, 2 * KT2 - 2)
                if has(i, -1, B - 2):
                    pack(two, i + 1, 0)
                    pack(two, i + 1, 1)
                max_rows(two, i, 3 * KT2 - 2)
                if has(i, -1, B - 2):
                    pack(two, i + 1, 2)

            loops(sp, second_loop, True)
            sp.wait_ge(stored.sem, stored.at(B - 1, 16))

        @block.gpsimd
        def _(pool):
            for n, (x, value) in enumerate(((w_p1[:, :, :], 0.0), (w_2a[:, :, :, :], 0.0), (xS[KC:KP, :, :], 0.0),
                                            (v1[:, :, :, :], 0.0), (v2[:, :, :, :], 0.0), (kpack[KC:KP, :, :], 0.0),
                                            (yA[KC:KP, :, :], 0.0), (v1[:, :, :, D:D + 1], 1.0),
                                            (v2[:, :, :, D:D + 1], 1.0), (kpack[6 * D:6 * D + 3, :, :], 1.0),
                                            (yA[KC:KC + 1, :, :], 1.0))):
                if n:
                    pool.wait_ge(setup_pool.sem, n)
                nc.gpsimd.memset(x, value).then_inc(setup_pool.sem, 1)
            for m in range(2, 4):
                pool.wait_ge(sc_rest.sem, m - 1)
                nc.gpsimd.tensor_copy(piece[:, m, 1, 0:SC], rest[:, m, 0:SC]).then_inc(sc_mid.sem, 1)
                pool.wait_ge(sc_mid.sem, m - 1)
                nc.gpsimd.tensor_tensor(piece[:, m, 2, 0:SC], rest[:, m, 0:SC], piece[:, m, 1, 0:SC],
                                        ALU.subtract).then_inc(sc_pieces.sem, 1)
            pool.wait_ge(loads.sem, 16 * NLOAD)

            def load_x(j):
                front.filled(pool, j - 3, F["tok"])
                front.emptied(pool, j - 3, F["proj"] + 1)
                pool.dma_start(pT[:, :, :], A["x"][j]).then_inc(x_in.sem, 16)
                pool.dma_start(hin[IMG - P:P, 1, :], A["txt"][j, 0:2 * P - IMG, :]).then_inc(x_in.sem, 16)
                pool.dma_start(hin[:, 2, :], A["txt"][j, 2 * P - IMG:TXT, :]).then_inc(x_in.sem, 16)

            def biased_input(j):
                front.emptied(pool, j - 2, F["tok"])
                pool.wait_ge(x_in.sem, x_in.at(j, 48))
                for t in range(T):
                    done = nc.gpsimd.tensor_tensor(hb[:, t, :], hin[:, t, :], b_p0[:, :], ALU.add)
                done.then_inc(hb_ready.sem, 1)

            def parts(att, ring, j):
                for m in range(4):
                    ring.emptied(pool, j - 1, ring.start["qk"] + m)
                    pool.wait_ge(att.scr_in.sem, att.scr_in.at(j, 0))
                    pool.sem_inc(gate_pool.sem)
                    nc.gpsimd.tensor_copy(piece[:, m, 1, :], rest[:, m, :]).then_inc(att.second.sem, 1)
                    pool.wait_ge(att.second.sem, att.second.at(j, m + 1))
                    nc.gpsimd.tensor_tensor(piece[:, m, 2, :], rest[:, m, :], piece[:, m, 1, :],
                                            ALU.subtract).then_inc(att.third.sem, 1)

            def first_loop(i):
                if has(i, -2, B - 3):
                    load_x(i + 2)
                if has(i, 1, B):
                    pool.wait_ge(lna_done.sem, lna_done.at(i - 1, 1))
                    pool.wait_ge(spilled.sem, spilled.at(i - 1, 0))
                    nc.gpsimd.tensor_tensor(hx[:, :, :], ha[:, :, :], xna[:, :, :], ALU.add).then_inc(hx_ready.sem, 1)
                if has(i, 0, B - 1):
                    back.emptied(pool, i, R["proj4"] + 1)
                    pool.wait_ge(hc_ready.sem, hc_ready.at(i, 1))
                    for t in range(T):
                        done = nc.gpsimd.tensor_tensor(hab[:, t, :], hc[:, t, :], b_p1[:, :], ALU.add)
                    done.then_inc(hab_ready.sem, 1)
                if has(i, -1, B - 2):
                    front.emptied(pool, i, F["out"] + 1)
                    pool.wait_ge(hab_ready.sem, hab_ready.at(i, 1))
                    pool.sem_inc(gate_pool.sem)
                    nc.gpsimd.tensor_copy(hc[:, :, :], h[:, :, :]).then_inc(hc_ready.sem, 1)
                    parts(one, front, i + 1)
                if has(i, -2, B - 3):
                    biased_input(i + 2)

            loops(pool, first_loop, False)
            parts(two, moe, 0)
            with pool.Fori(0, B - 1) as i:
                parts(two, moe, i + 1)
            pool.wait_ge(x_in.sem, x_in.at(B - 1, 48))

        @block.scalar
        def _(act):
            act.wait_ge(loads.sem, 16 * NLOAD)
            act.wait_ge(setup_dve.sem, SETUP_DVE)
            for m in range(2):
                act.wait_ge(setup_pe.sem, m + 1)
                nc.scalar.copy(piece[:, 2 + m, 0, 0:SC], lin[0:KC, m, 0:SC]).then_inc(sc_first.sem, 1)
            act.wait_ge(setup_pe.sem, 3)
            act.wait_ge(setup_pool.sem, SETUP_POOL)
            nc.scalar.copy(v1[0:TK1, KT1 - 1, :, 0:D],
                           mps[0:TK1, 0, 0:C].rearrange("p (h d) -> p h d", d=D)).then_inc(setup_act.sem, 1)

            def transposed(ring, i, step, dst):
                for k in range(2):
                    u = ring.start[step] + k
                    ring.filled(act, i, u)
                    nc.scalar.copy(dst[0:KC, k, 0:N], ring.at(u)[0:KC, 0:N]).then_inc(ring.free["act"].sem, 1)

            def hidden(ring, i, bias):
                for f in range(FT):
                    u = ring.start["hidden"] + f
                    ring.filled(act, i, u)
                    nc.scalar.activation(g[:, f, :], ring.at(u)[:, 0:N], ACT.Gelu,
                                         bias=b_in[:, f:f + 1] if bias else 0.0).then_inc(ring.free["act"].sem, 1)

            def first_parts(att, ring, j, i):
                for m in range(4):
                    u = ring.start["qk"] + m
                    ring.filled(act, i, u)
                    act.wait_ge(att.scr_in.sem, att.scr_in.at(j, 0))
                    nc.scalar.copy(piece[:, m, 0, :], ring.at(u)[0:KC, 0:N]).then_inc(att.first.sem, 1)

            def values(att, ring, j, i, nt):
                act.wait_ge(att.summed.sem, att.summed.at(j, 0))
                for k in range((nt + 1) // 2):
                    u = ring.start["values"] + k
                    ring.filled(act, i, u)
                    for s in range(min(2, nt - 2 * k)):
                        done = nc.scalar.copy(att.values[0:att.rows, 2 * k + s, :, 0:D],
                                              tiles2(ring.at(u))[0:att.rows, s, :].rearrange("p (h d) -> p h d", d=D))
                    done.then_inc(ring.free["act"].sem, 1)

            def first_step(j, i, step):
                if step == "tok":
                    front.filled(act, i, F["tok"])
                    act.wait_ge(x_in.sem, x_in.at(j, 48))
                    b = tiles2(front.at(F["tok"]))
                    nc.scalar.copy(hin[:, 0, :], b[0:P, 0, :])
                    nc.scalar.copy(hin[0:IMG - P, 1, :], b[0:IMG - P, 1, :]).then_inc(front.free["act"].sem, 1)
                elif step in ("t1", "t2"):
                    transposed(front, i, step, xT)
                elif step == "zv":
                    act.wait_ge(nmz_ready.sem, nmz_ready.at(j, 1))
                    nc.scalar.activation(zexp[:, :], front.at(F["zv"])[0:H, 0:N], ACT.Exp, bias=nmz[:, 0:1],
                                         accum_out=zsum[:, 0:1]).then_inc(zexp_ready.sem, 1)
                    for k, tiles in ((0, slice(0, 2)), (1, slice(2, 3))):
                        u = F["zv"] + 1 + k
                        front.filled(act, i, u)
                        nc.scalar.copy(vz[0:P, tiles, 0:C], tiles2(front.at(u))[0:P, 0:2 - k]).then_inc(front.free["act"].sem, 1)
                elif step == "inv":
                    transposed(front, i, step, aT)
                elif step == "hidden":
                    hidden(front, i, True)
                elif step == "t3":
                    transposed(front, i, step, xS)
                elif step == "qk":
                    first_parts(one, front, j, i)
                elif step == "values":
                    values(one, front, j, i, 4)
                elif step == "t4":
                    transposed(back, i, step, xTa)
                elif step == "exp":
                    act.wait_ge(lg_ready.sem, lg_ready.at(j, 1))
                    nc.scalar.activation(pr[:, :, :], lg[:, :, :], ACT.Exp).then_inc(pe_ready.sem, 1)
                elif step == "t5":
                    act.wait_ge(spilled.sem, spilled.at(j, 0))
                    for k in range(2):
                        u = R["t5"] + k
                        back.filled(act, i, u)
                        nc.scalar.activation(yA[0:KC, k, :], back.at(u)[0:KC, 0:N], ACT.Identity,
                                             bias=beta[:, k:k + 1], scale=gamma[:, k:k + 1]).then_inc(back.free["act"].sem, 1)

            def second_step(j, i, step):
                if step == "hidden":
                    moe.filled(act, i, M["out"] + 1)
                    hidden(moe, i, False)
                elif step == "qk":
                    first_parts(two, moe, j, i)
                elif step == "values":
                    values(two, moe, j, i, 3)
                elif step == "gate":
                    act.wait_ge(fin_ready.sem, fin_ready.at(j, 0))
                    for k, tiles in ((0, slice(0, 2)), (1, slice(2, 3))):
                        u = O["gate"] + k
                        last.filled(act, i, u)
                        nc.scalar.copy(gm[:, tiles, :], tiles2(last.at(u))[0:P, 0:2 - k]).then_inc(last.free["act"].sem, 1)

            def quad(att, i, slot):
                if slot == "end":
                    return
                for n in range(4 * slot, 4 * slot + 4):
                    act.wait_ge(att.scored.sem, att.scored.at(i, n + 1))
                    act.wait_ge(att.summed.sem, att.summed.at(i, n - NP + 1))
                    nc.scalar.activation(prob[0:att.rows, n % NP, :], sps[0:att.rows, n % 3, 0:N], ACT.Exp,
                                         scale=SCALE).then_inc(att.exped.sem, 1)

            def maxima(att, i, b, slot):
                pass

            def rows(att, i, b, slot):
                q, u = att.maxima(slot)[0], att.ring.start["row", slot]
                att.ring.filled(act, i, u)
                act.wait_ge(att.rows_in.sem, att.rows_in.at(b, 48 * q))
                nc.scalar.copy(mT[:, :], att.ring.at(u)[0:12, 0:N // 2].bitcast(bf16)).then_inc(att.ring.free["act"].sem, 1)

            loops(act, lambda i: iteration(act, "act", i, False, quad, maxima, rows, first_step), False)
            loops(act, lambda i: iteration(act, "act", i, True, quad, maxima, rows, second_step), True)

        @block.vector
        def _(dve):
            for x in (xT[KC:KP, :, :], aT[KC:KP, :, :], vz[KC:KP, :, :], of[64:KP, :, :, :], rc[:, :], sel[:, :],
                      gate[:, :], qpack[KC:KP, :, :], prob[KC:KP, :, :]):
                nc.vector.memset(x, 0.0).then_inc(setup_dve.sem, 1)
            dve.wait_ge(loads.sem, 16 * NLOAD)
            nc.vector.tensor_copy(identb[:, :], ident[:, :]).then_inc(setup_dve.sem, 1)
            nc.vector.tensor_tensor(w_2[:, 0], w_2[:, 0], w_2[:, 1], ALU.add).then_inc(setup_dve.sem, 1)
            nc.vector.tensor_tensor(w_2a[:, 0], w_2a[:, 0], w_2a[:, 1], ALU.add).then_inc(setup_dve.sem, 1)
            nc.vector.tensor_tensor(b_2[:, 0], b_2[:, 0], b_2[:, 1], ALU.add).then_inc(setup_dve.sem, 1)
            for m in range(2):
                dve.wait_ge(sc_first.sem, m + 1)
                nc.vector.tensor_tensor(rest[:, 2 + m, 0:SC], lin[0:KC, m, 0:SC], piece[:, 2 + m, 0, 0:SC],
                                        ALU.subtract).then_inc(sc_rest.sem, 1)
            dve.wait_ge(setup_dve.sem, SETUP_DVE)
            dve.wait_ge(sc_pieces.sem, 2)
            links = [0]

            def link(ins):
                links[0] += 1
                ins.then_inc(dve_link.sem, 1)
                dve.wait_ge(dve_link.sem, links[0])

            def restart():
                links[0] = 0
                dve.sem_clear(dve_link.sem)

            def layernorm(src, dst, eps, signals):
                for t in range(T):
                    done = nc.vector.bn_stats(st[:, t, :], src[:, t, :])
                link(done)
                for t in range(T):
                    done = nc.vector.bn_aggr(mv[:, t, :], st[:, t, :])
                link(done)
                link(nc.vector.tensor_scalar(var[:, :], mv[:, :, 1], eps, None, ALU.add))
                link(nc.vector.tensor_scalar(rs[:, :].bitcast(i32), var[:, :].bitcast(i32), -0.5, 1597463007.0,
                                             ALU.mult, ALU.add))
                for _ in range(3):
                    link(nc.vector.tensor_tensor(nt[:, :], rs[:, :], rs[:, :], ALU.mult))
                    link(nc.vector.scalar_tensor_tensor(nt[:, :], nt[:, :], -0.5, var[:, :], ALU.mult, ALU.mult))
                    link(nc.vector.scalar_tensor_tensor(rs[:, :], nt[:, :], 1.5, rs[:, :], ALU.add, ALU.mult))
                for t in range(T):
                    done = nc.vector.tensor_scalar(dst[:, t, :], src[:, t, :], mv[:, t, 0:1], rs[:, t:t + 1],
                                                   ALU.subtract, ALU.mult)
                done.then_inc(signals.sem, 1)

            def residual(ring, i, step, dst, add):
                u = ring.start[step]
                for k in range(2):
                    ring.filled(dve, i, u + k)
                    t = slice(0, 2) if k == 0 else slice(2, 3)
                    nc.vector.tensor_tensor(dst[:, t, :], tiles2(ring.at(u + k))[0:P, 0:2 - k, :], add[:, t, :],
                                            ALU.add).then_inc(ring.free["dve"].sem, 1)
                ring.emptied(dve, i, u + 1)

            def rests(att, ring, j, i):
                for m in range(4):
                    u = ring.start["qk"] + m
                    ring.filled(dve, i, u)
                    dve.wait_ge(att.first.sem, att.first.at(j, m + 1))
                    dve.wait_ge(att.third.sem, att.third.at(j, 0))
                    nc.vector.tensor_tensor(rest[:, m, :], ring.at(u)[0:KC, 0:N], piece[:, m, 0, :],
                                            ALU.subtract).then_inc(ring.free["dve"].sem, 1)

            def first_step(j, i, step):
                free = front.free["dve"].sem
                if step == "tok":
                    front.emptied(dve, i, F["tok"])
                    layernorm(hin, xn, 1e-5, ln_done)
                elif step == "zv":
                    front.filled(dve, i, F["zv"])
                    nc.vector.tensor_reduce(nmz[:, 0:1], front.at(F["zv"])[0:H, 0:N], AX.X, ALU.max,
                                            negate=True).then_inc(nmz_ready.sem, 1)
                    dve.wait_ge(zexp_ready.sem, zexp_ready.at(j, 1))
                    link(nc.vector.reciprocal(zrec[:, :], zsum[:, :]))
                    nc.vector.tensor_scalar(zexp[:, :], zexp[:, :], zrec[:, 0:1], 1.0 / N, ALU.mult,
                                            ALU.mult).then_inc(free, 1)
                elif step == "zt":
                    front.filled(dve, i, F["zt"])
                    nc.vector.tensor_copy(vz[0:P, :, C:C + H], front.at(F["zt"])[0:P, 0:T * H]
                                          .rearrange("p (t h) -> p t h", t=T)).then_inc(free, 1)
                elif step == "dft":
                    vr, vi = (front.at(F["dft"] + s)[0:FW].rearrange("p (f c) -> p f c", f=2) for s in range(2))
                    front.filled(dve, i, F["dft"])
                    link(nc.vector.tensor_copy(zf[:, 0, :, :], vr[:, :, C:C + H]))
                    front.filled(dve, i, F["dft"] + 1)
                    link(nc.vector.tensor_copy(zf[:, 1, :, :], vi[:, :, C:C + H]))

                    def times(dst, v, part):
                        for f in range(2):
                            done = nc.vector.tensor_tensor(
                                dst[:, f, :].rearrange("p (h d) -> p h d", d=D),
                                v[:, f, 0:C].rearrange("p (h d) -> p h d", d=D),
                                zf[:, part, f, :].rearrange("p (h a) -> p h a", a=1).broadcast_to([FW, H, D]), ALU.mult)
                        return done

                    times(ta, vr, 0)
                    link(times(tb, vi, 1))
                    link(nc.vector.tensor_tensor(of[0:FW, 0], ta[:, :, :], tb[:, :, :], ALU.add))
                    times(ta, vi, 0).then_inc(free, 1)
                    times(tb, vr, 1).then_inc(free, 1)
                    front.emptied(dve, i, F["dft"] + 1)
                    nc.vector.tensor_tensor(of[0:FW, 1], ta[:, :, :], tb[:, :, :], ALU.subtract).then_inc(of_ready.sem, 1)
                elif step == "proj":
                    dve.wait_ge(hb_ready.sem, hb_ready.at(j, 1))
                    residual(front, i, step, h, hb)
                    layernorm(h, xn, 1e-5, ln_done)
                elif step == "out":
                    residual(front, i, step, h, h)
                    layernorm(h, xn, 1e-5, ln_done)
                elif step == "qk":
                    rests(one, front, j, i)
                elif step == "den":
                    invert(back, i)
                elif step == "norm":
                    normalise(one, i)
                elif step == "proj4":
                    dve.wait_ge(hab_ready.sem, hab_ready.at(j, 1))
                    dve.wait_ge(hx_ready.sem, hx_ready.at(j, 0))
                    residual(back, i, step, ha, hab)
                    layernorm(ha, xna, 1e-5, lna_done)
                elif step == "ln5":
                    dve.wait_ge(lna_done.sem, lna_done.at(j, 1))
                    layernorm(xna, xn5, 1e-6, lna_done)
                elif step == "log":
                    u = R["log"]
                    back.filled(dve, i, u)
                    lgp = back.at(u)[0:P, 0:T * E].rearrange("p (t e) -> p t e", t=T)
                    link(nc.vector.tensor_reduce(lmx[:, :], lgp, AX.X, ALU.max))
                    for t in range(T):
                        done = nc.vector.tensor_scalar(lg[:, t, :], lgp[:, t, :], lmx[:, t:t + 1], None, ALU.subtract)
                    done.then_inc(back.free["dve"].sem, 1)
                    back.emptied(dve, i, u)
                    nc.vector.tensor_copy(nta[:, :], lmx[:, :]).then_inc(lg_ready.sem, 1)
                elif step == "prob":
                    dve.wait_ge(pe_ready.sem, pe_ready.at(j, 1))
                    link(nc.vector.tensor_reduce(lmx[:, :], pr[:, :, :], AX.X, ALU.add))
                    link(nc.vector.reciprocal(nta[:, :], lmx[:, :]))
                    for t in range(T):
                        done = nc.vector.tensor_scalar(pr[:, t, :], pr[:, t, :], nta[:, t:t + 1], None, ALU.mult)
                    done.then_inc(pr_ready.sem, 1)
                elif step == "prt":
                    u = R["prt"]
                    back.filled(dve, i, u)
                    dve.wait_ge(spilled.sem, spilled.at(j, 0))
                    nc.vector.tensor_copy(prT[:, :], back.at(u)[0:E, 0:N]).then_inc(back.free["dve"].sem, 1)

            def invert(ring, i):
                u = ring.start["den"]
                ring.filled(dve, i, u)
                nc.vector.reciprocal(rc[0:H, :], ring.at(u)[0:H, 0:N]).then_inc(ring.free["dve"].sem, 1)

            def normalise(att, i):
                ring, u = att.ring, att.ring.start["norm"]
                for q in range(GROUPS):
                    ring.filled(dve, i, u + q)
                    nc.vector.tensor_tensor(av[:, q, :], av[:, q, :], ring.at(u + q)[:, 0:N],
                                            ALU.mult).then_inc(ring.free["dve"].sem, 1)

            def quad(att, i, slot):
                n = GROUPS * att.kt if slot == "end" else slot
                if n and n % att.kt == 0:
                    q = n // att.kt - 1
                    dve.wait_ge(att.summed.sem, att.summed.at(i, 4 * n))
                    nc.vector.tensor_copy(av[:, q, :], aps[:, 0:N]).then_inc(att.copied.sem, 1)

            def maxima(att, i, b, slot):
                ring, u0 = att.ring, att.ring.start["max", slot]
                q, units, complete = att.maxima(slot)
                for u, n in enumerate(units, u0):
                    hd, t, s = n // (T * att.halves), n // att.halves % T, n % att.halves
                    ring.filled(dve, i, u)
                    nc.vector.tensor_reduce(mxh[:, hd, t, s:s + 1], ring.at(u)[0:P, 0:att.width], AX.X, ALU.max,
                                            negate=att.halves == 1).then_inc(ring.free["dve"].sem, 1)
                if not complete:
                    return
                ring.emptied(dve, i, u)
                src = [mxh[:, :, :, s].rearrange("p h t -> p t h") for s in range(2)]
                if att.halves == 2:
                    link(nc.vector.tensor_tensor(mr[:, :, :], src[0], src[1], ALU.max))
                    link(nc.vector.tensor_scalar(mx[:, :, :], mr[:, :, :], -1.0, None, ALU.mult))
                else:
                    link(nc.vector.tensor_copy(mx[:, :, :], src[0]))
                link(nc.vector.tensor_copy(mp[:, :, 0, :], mx[:, :, :]))
                link(nc.vector.tensor_tensor(mr[:, :, :], mx[:, :, :], mp[:, :, 0, :], ALU.subtract))
                link(nc.vector.tensor_copy(mp[:, :, 1, :], mr[:, :, :]))
                nc.vector.tensor_tensor(mp[:, :, 2, :], mr[:, :, :], mp[:, :, 1, :], ALU.subtract).then_inc(att.maxed.sem, 1)

            def rows(att, i, b, slot):
                pass

            def first_loop(i):
                restart()
                iteration(dve, "dve", i, False, quad, maxima, rows, first_step)

            loops(dve, first_loop, False)

            restart()
            nc.vector.memset(work[:, N:], 2.0)
            dve.wait_ge(picks_in.sem, 16)
            link(nc.vector.tensor_copy(work[:, 0:N], pall[:, :]))
            for _ in range(ROUNDS):
                link(nc.vector.max(top8[:, :], work[:, :]))
                link(nc.vector.match_replace(work[:, :], top8[:, :], work[:, :], -1.0))
            nc.vector.tensor_scalar(selall[:, :], work[:, 0:N], 0.0, None, ALU.is_lt).then_inc(picked.sem, 1)
            dve.wait_ge(picked.sem, 1)
            nc.vector.tensor_tensor(gateall[:, :], selall[:, :], pall[:, :], ALU.mult).then_inc(picked.sem, 1)

            def second_step(j, i, step):
                if step == "count":
                    dve.wait_ge(moe_in.sem, moe_in.at(j, 32))
                    for k in range(2):
                        u = M["count"] + k
                        moe.filled(dve, i, u)
                        nc.vector.tensor_tensor(yT[:, k, :], yT[:, k, :], moe.at(u)[:, 0:N],
                                                ALU.mult).then_inc(moe.free["dve"].sem, 1)
                elif step == "qk":
                    rests(two, moe, j, i)
                elif step == "out":
                    for k in range(2):
                        u = M["out"] + k
                        moe.filled(dve, i, u)
                        for t in range(2 - k):
                            done = nc.vector.tensor_tensor(acc[:, 2 * k + t, :], tiles2(moe.at(u))[0:P, t, :], b_2[:, 0, :], ALU.add)
                        done.then_inc(moe.free["dve"].sem, 1)
                elif step == "den":
                    invert(last, i)
                elif step == "norm":
                    normalise(two, i)
                elif step == "final":
                    residual(last, i, step, acc, acc)
                    last.emptied(dve, i, O["gate"] + 1)
                    dve.wait_ge(tail_in.sem, tail_in.at(j, 32))
                    dve.wait_ge(stored.sem, stored.at(j, 0))
                    link(nc.vector.tensor_tensor(fin[:, :, :], acc[:, :, :], gm[:, :, :], ALU.mult))
                    nc.vector.tensor_tensor(fin[:, :, :], fin[:, :, :], hxb[:, :, :], ALU.add).then_inc(fin_ready.sem, 1)

            def second_loop(i):
                restart()
                iteration(dve, "dve", i, True, quad, maxima, rows, second_step)

            loops(dve, second_loop, True)

        @block.tensor
        def _(pe):
            mm = nc.tensor.matmul
            pe.wait_ge(loads.sem, 16 * NLOAD)
            pe.wait_ge(setup_dve.sem, SETUP_DVE)
            pe.wait_ge(setup_pool.sem, SETUP_POOL)
            for m in range(2):
                for k in range(2):
                    done = mm(lin[0:KC, m, 0:SC], w_qkv[:, k, C + m * KC:C + (m + 1) * KC], xS[:, k, N:NK1],
                              start=k == 0, stop=k == 1)
                done.then_inc(setup_pe.sem, 1)
            for k in range(2):
                done = mm(mps[0:TK1, 0, 0:C], xS[:, k, (KT1 - 1) * TK1:NK1], w_qkv[:, k, 2 * C:], start=k == 0, stop=k == 1)
            done.then_inc(setup_pe.sem, 1)
            pe.wait_ge(setup_act.sem, 1)
            pe.wait_ge(sc_rest.sem, 2)
            pe.wait_ge(sc_pack.sem, 16 * 6)

            def transposes(ring, j, i, step, src, signals, n):
                pe.wait_ge(signals.sem, signals.at(j, n))
                for c in range(2):
                    b = ring.bank(pe, i, ring.start[step] + c)
                    for t in range(T):
                        done = nc.tensor.transpose(b[0:KC, t * P:(t + 1) * P],
                                                   src[:, t, c * KC:(c + 1) * KC], ident[0:P, 0:P])
                    done.then_inc(ring.full.sem, 1)

            def by_token(ring, i, u, acts, weights, rows, nt):
                for t in range(nt):
                    if t % 2 == 0:
                        b = ring.bank(pe, i, u + t // 2)
                    for k, (x, w) in enumerate(zip(acts, weights)):
                        done = mm(tiles2(b)[0:rows, t % 2, :], x[:, t * rows:(t + 1) * rows], w,
                                  start=k == 0, stop=k == len(acts) - 1)
                    if t % 2 == 1 or t == nt - 1:
                        done.then_inc(ring.full.sem, 1)

            def by_channel(ring, i, step, x, w, c0, size, count):
                for m in range(count):
                    b = ring.bank(pe, i, ring.start[step] + m)
                    c = c0 + m * size
                    for k in range(2):
                        done = mm(b[0:size, 0:N], w[:, k, c:c + size], x[:, k, 0:N], start=k == 0, stop=k == 1)
                    done.then_inc(ring.full.sem, 1)

            def quad(att, i, slot):
                kt, rows = att.kt, att.rows
                n4 = GROUPS * kt if slot == "end" else slot
                if n4 == 0:
                    ring = front if att is one else moe
                    ring.emptied(pe, i - 1, ring.start["values"] + 1)
                if n4 < GROUPS * kt:
                    q, k = divmod(n4, kt)
                    if k == 0:
                        pe.wait_ge(att.rows_in.sem, att.rows_in.at(i, 48 * (q + 1)))
                    for n in range(4 * n4, 4 * n4 + 4):
                        pe.wait_ge(att.exped.sem, att.exped.at(i, n - 2))
                        mm(sps[0:rows, n % 3, 0:N], kpack[:, 4 * q + n % 4, k * rows:(k + 1) * rows],
                           qpack[:, 4 * q + n % 4, :], start=True, stop=True).then_inc(att.scored.sem, 1)
                if n4 > 0:
                    q, k = divmod(n4 - 1, kt)
                    if k == 0:
                        pe.wait_ge(att.copied.sem, att.copied.at(i, q))
                    for n in range(4 * n4 - 4, 4 * n4):
                        j = n % 4
                        pe.wait_ge(att.exped.sem, att.exped.at(i, n + 1))
                        mm(aps[32 * j:32 * j + 32, 0:N], att.values[:, k, 4 * q + j, :], prob[:, n % NP, :],
                           start=k == 0, stop=k == kt - 1).then_inc(att.summed.sem, 1)

            def maxima(att, i, b, slot):
                q, units, complete = att.maxima(slot)
                if units[0] == 0:
                    pe.wait_ge(att.pack_in[q].sem, att.pack_in[q].at(b, 192))
                for u, n in enumerate(units, att.ring.start["max", slot]):
                    hd, t, s = n // (T * att.halves), n // att.halves % T, n % att.halves
                    bank = att.ring.bank(pe, i, u)
                    mm(bank[0:P, 0:att.width], qpack[0:6 * D, 4 * q + hd, t * P:(t + 1) * P],
                       kpack[0:6 * D, 4 * q + hd, s * att.width:(s + 1) * att.width],
                       start=True, stop=True).then_inc(att.ring.full.sem, 1)

            def rows(att, i, b, slot):
                bank = att.ring.bank(pe, i, att.ring.start["row", slot])
                pe.wait_ge(att.maxed.sem, att.maxed.at(b, att.maxima(slot)[0] + 1))
                pe.sem_inc(gate_pe.sem)
                for t in range(T):
                    done = nc.tensor.transpose(bank[0:12, t * (P // 2):(t + 1) * (P // 2)].bitcast(bf16),
                                               mp[:, t].rearrange("p s h -> p (s h)"), identb[0:P, 0:P])
                done.then_inc(att.ring.full.sem, 1)

            def denominators(att, j, i):
                b = att.ring.bank(pe, i, att.ring.start["den"])
                for q in range(GROUPS):
                    pe.wait_ge(att.copied.sem, att.copied.at(j, q + 1))
                    done = mm(b[0:H, 0:N], gather[:, q, :], av[:, q, :], start=q == 0, stop=q == GROUPS - 1)
                done.then_inc(att.ring.full.sem, 1)

            def spread_out(ring, i):
                ring.emptied(pe, i, ring.start["den"])
                for q in range(GROUPS):
                    b = ring.bank(pe, i, ring.start["norm"] + q)
                    mm(b[:, 0:N], spread[:, q, :], rc[:, :], start=True, stop=True).then_inc(ring.full.sem, 1)

            def pair(x, w, c0=0):
                return [x[:, k, :] for k in range(2)], [w[:, k, c0:] for k in range(2)]

            def first_step(j, i, step):
                u = F.get(step, R.get(step))
                if step == "tok":
                    pe.wait_ge(x_in.sem, x_in.at(j, 48))
                    b = front.bank(pe, i, u)
                    for t, n in ((0, P), (1, IMG - P)):
                        for k in range(2):
                            done = mm(tiles2(b)[0:n, t, :], pT[:, k, t * P:t * P + n], w_tok[:, k, :],
                                      start=k == 0, stop=k == 1)
                    done.then_inc(front.full.sem, 1)
                elif step == "t1":
                    transposes(front, j, i, step, xn, ln_done, 1)
                elif step == "zv":
                    front.emptied(pe, i, F["t1"] + 1)
                    b = front.bank(pe, i, u)
                    for k in range(2):
                        done = mm(b[0:H, 0:N], w_a[:, k, :], xT[:, k, :], start=k == 0, stop=k == 1)
                    done.then_inc(front.full.sem, 1)
                    by_token(front, i, u + 1, *pair(xT, w_v0), P, T)
                elif step == "zt":
                    b = front.bank(pe, i, u)
                    front.emptied(pe, i, F["zv"])
                    pe.sem_inc(gate_pe.sem)
                    for t in range(T):
                        done = nc.tensor.transpose(b[0:P, t * H:(t + 1) * H], zexp[:, t * P:(t + 1) * P], ident[0:H, 0:H])
                    done.then_inc(front.full.sem, 1)
                elif step == "dft":
                    for part in range(2):
                        b = front.bank(pe, i, u + part)
                        front.emptied(pe, i, F["zt"])
                        for f in range(2):
                            for t in range(T):
                                done = mm(b[0:FW, 256 * f:256 * f + C + H], dft[:, t, part, f, :], vz[:, t, :],
                                          start=t == 0, stop=t == T - 1)
                        done.then_inc(front.full.sem, 1)
                elif step == "inv":
                    pe.wait_ge(of_ready.sem, of_ready.at(j, 1))
                    for m in range(2):
                        b = front.bank(pe, i, u + m)
                        for n in range(4):
                            done = mm(b[0:KC, 0:N], of[:, n // 2, n % 2, m * KC:(m + 1) * KC], idft[:, n // 2, n % 2, :],
                                      start=n == 0, stop=n == 3)
                        done.then_inc(front.full.sem, 1)
                elif step == "proj":
                    front.emptied(pe, i, F["inv"] + 1)
                    by_token(front, i, u, *pair(aT, w_p0), P, T)
                elif step == "t2":
                    transposes(front, j, i, step, xn, ln_done, 2)
                elif step == "hidden":
                    front.emptied(pe, i, F["t2"] + 1)
                    by_channel(front, i, step, xT, w_in, 0, 128, FT)
                elif step == "out":
                    front.emptied(pe, i, F["hidden"] + FT - 1)
                    by_token(front, i, u, [g[:, k, :] for k in range(FT)], [w_out[:, k, :] for k in range(FT)], P, T)
                elif step == "t3":
                    transposes(front, j, i, step, xn, ln_done, 3)
                elif step == "qk":
                    front.emptied(pe, i, F["t3"] + 1)
                    by_channel(front, i, step, xS, w_qkv, 0, KC, 4)
                elif step == "values":
                    by_token(front, i, u, *pair(xS, w_qkv, 2 * C), TK1, 4)
                elif step == "den":
                    denominators(one, j, i)
                elif step == "norm":
                    spread_out(back, i)
                elif step == "proj4":
                    back.emptied(pe, i, R["norm"] + GROUPS - 1)
                    by_token(back, i, u, [av[:, k, :] for k in range(GROUPS)], [w_p1[:, k, :] for k in range(GROUPS)], P, T)
                elif step == "t4":
                    transposes(back, j, i, step, xna, lna_done, 1)
                elif step == "log":
                    back.emptied(pe, i, R["t4"] + 1)
                    b = back.bank(pe, i, u)
                    for t in range(T):
                        for k in range(2):
                            done = mm(b[0:P, t * E:(t + 1) * E], xTa[:, k, t * P:(t + 1) * P], w_r[:, k, :],
                                      start=k == 0, stop=k == 1)
                    done.then_inc(back.full.sem, 1)
                elif step == "prt":
                    b = back.bank(pe, i, u)
                    pe.wait_ge(pr_ready.sem, pr_ready.at(j, 1))
                    for t in range(T):
                        done = nc.tensor.transpose(b[0:E, t * P:(t + 1) * P], pr[:, t, :], ident[0:P, 0:P])
                    done.then_inc(back.full.sem, 1)
                elif step == "t5":
                    transposes(back, j, i, step, xn5, lna_done, 2)

            def second_step(j, i, step):
                if step == "count":
                    pe.wait_ge(moe_in.sem, moe_in.at(j, 32))
                    for m in range(2):
                        b = moe.bank(pe, i, M["count"] + m)
                        mm(b[:, 0:N], emask[:, m * KP:(m + 1) * KP], sel[:, :], start=True, stop=True).then_inc(moe.full.sem, 1)
                elif step == "qk":
                    moe.emptied(pe, i, M["count"] + 1)
                    by_channel(moe, i, step, yT, w_1, FH, KC, 4)
                elif step == "hidden":
                    by_channel(moe, i, step, yT, w_1, 0, 128, FT)
                elif step == "values":
                    by_token(moe, i, M["values"], *pair(yT, w_1, FH + 2 * C), P, T)
                elif step == "out":
                    moe.emptied(pe, i - 1, M["hidden"] + FT - 1)
                    by_token(moe, i, M["out"], [g[:, f, :] for f in range(FT)], [w_2[:, 0, f, :] for f in range(FT)], P, T)
                elif step == "den":
                    denominators(two, j, i)
                elif step == "norm":
                    spread_out(last, i)
                elif step == "gate":
                    pe.wait_ge(tail_in.sem, tail_in.at(j, 32))
                    by_token(last, i, O["gate"], [gate[:, :]], [emaskc[:, :]], P, T)
                elif step == "final":
                    last.emptied(pe, i, O["norm"] + GROUPS - 1)
                    by_token(last, i, O["final"], [av[:, k, :] for k in range(GROUPS)],
                             [w_2a[:, 0, k, :] for k in range(GROUPS)], P, T)

            loops(pe, lambda i: iteration(pe, "pe", i, False, quad, maxima, rows, first_step), False)
            loops(pe, lambda i: iteration(pe, "pe", i, True, quad, maxima, rows, second_step), True)


def kernel(**inputs):
    import numpy as _np
    import concourse.bacc as _bacc
    from concourse import mybir as _mybir
    from concourse.bass_utils import run_bass_kernel_spmd as _run

    a = {k: _np.asarray(v) for k, v in inputs.items()}

    def rows(w, r):
        return w.reshape(-1, r, w.shape[1]).transpose(1, 0, 2)

    def padded(w, axis=0):
        pad = [(0, 0)] * w.ndim
        pad[axis] = (0, KP - w.shape[axis])
        return _np.pad(w, pad)

    nh = a["x"].shape[2] // 16
    k = _np.minimum(_np.arange(2 * FW), NF)
    live = (_np.arange(2 * FW) < NF)[:, None]
    ang = 2 * _np.pi * ((k[:, None] * _np.arange(N)[None, :]) % N) / N
    both = _np.stack([_np.cos(ang) * live, _np.sin(ang) * live * ((k % (N // 2)) != 0)[:, None]])
    weight = _np.where((k % (N // 2)) == 0, 1.0, 2.0)[:, None]
    dft = both.reshape(2, 2, FW, T, P).transpose(4, 3, 0, 1, 2)
    idft = (both * weight / N).reshape(2, 2, FW, N).transpose(2, 0, 1, 3)
    width = C // 2 ** (E - 1 - _np.arange(E))
    emask = (_np.arange(C)[None, :] < width[:, None])
    gather, spread = _np.zeros((128, GROUPS, H)), _np.zeros((H, GROUPS, 128))
    for hd in range(H):
        r = 32 * (hd % 4)
        gather[r + D, hd // 4, hd] = 1.0
        spread[hd, hd // 4, r:r + 32] = 1.0
    bias = _np.zeros((1, 2, FH + 3 * C), _np.float32)
    bias[0, 1] = a["L1_ffn_b1"].reshape(-1)
    arrays = {
        "x": a["x"].reshape(B, nh, 16, nh, 16).transpose(0, 2, 4, 1, 3).reshape(B, 2, 128, IMG).transpose(0, 2, 1, 3),
        "txt": a["txt"],
        "w_tok": rows(a["L0_tok_W"].T, 128),
        "w_a": padded(rows(a["L0_attn_W_A"], KC)),
        "w_v0": padded(rows(a["L0_attn_W_V"], KC)),
        "w_p0": padded(rows(a["L0_attn_W_proj"], KC)),
        "b_p0": a["L0_attn_b_proj"],
        "w_in": padded(rows(a["L0_ffn_in_weight"].T, KC)),
        "b_in": a["L0_ffn_in_bias"].reshape(FT, 128).T,
        "w_out": rows(a["L0_ffn_out_weight"], 128),
        "sc": rows(a["L1_attn_sc_token"][0].T, KC),
        "w_qkv": padded(rows(a["L1_attn_W_qkv"], KC)),
        "w_p1": a["L1_attn_W_proj"],
        "b_p1": a["L1_attn_b_proj"],
        "w_r": rows(a["L1_ffn_w_router"].T, KC),
        "gamma": a["L1_ffn_gamma1"].reshape(2, KC).T,
        "beta": a["L1_ffn_beta1"].reshape(2, KC).T,
        "w_1": padded(_np.concatenate([rows(a["L1_ffn_w1"].T, KC), bias], 0)),
        "w_2": a["L1_ffn_w2"][:, :FH].reshape(2, C, FT, 128).transpose(3, 0, 2, 1),
        "w_2a": a["L1_ffn_w2"][:, FH:].reshape(2, C, C).transpose(0, 2, 1),
        "b_2": a["L1_ffn_b2"].reshape(2, C),
        "ident": _np.eye(128, dtype=_np.float32),
        "dft": padded(dft.astype(_np.float32)),
        "idft": padded(idft.astype(_np.float32)),
        "spread": padded(spread.astype(_np.float32)),
        "gather": gather.astype(_np.float32),
        "emask": padded(emask.astype(_np.float32)),
        "emask2": padded(_np.concatenate([padded(emask[:, :KC], 1), padded(_np.concatenate([emask[:, KC:], emask[:, :1]], 1), 1)],
                                         1).astype(_np.float32)),
    }
    nc = _bacc.Bacc("TRN2", target_bir_lowering=False, num_devices=1)
    ins, aps = {}, {}
    for name, v in arrays.items():
        v = _np.ascontiguousarray(v)
        ins[f"in_{name}"] = v
        aps[name] = nc.dram_tensor(f"in_{name}", v.shape, _mybir.dt.from_np(v.dtype), kind="ExternalInput").ap()
    aps["out"] = nc.dram_tensor("out_0", (B, N, C), _mybir.dt.float32, kind="ExternalOutput").ap()
    build(nc, aps)
    r = _run(nc, [ins], core_ids=[0])
    return r.results[0]["out_0"]
```
